# Optimizing a Trainium2 kernel written in Bass

```python
import numpy as np
import jax
import jax.numpy as jnp

def _softmax(x, axis=-1):
    return jax.nn.softmax(x, axis=axis)

def _gelu(x):
    return jax.nn.gelu(x, approximate=True)

def _silu(x):
    return jax.nn.silu(x)

def _sigmoid(x):
    return jax.nn.sigmoid(x)

def _layernorm(x, axis=-1, eps=1e-05):
    m = jnp.mean(x, axis=axis, keepdims=True)
    v = jnp.var(x, axis=axis, keepdims=True)
    return (x - m) / jnp.sqrt(v + eps)

def _scatter_add(tgt, idx, src, axis=0):
    return tgt.at[idx].add(src)

def _segment_sum(src, seg, n):
    return jax.ops.segment_sum(src, seg, n)
kernel_name = 'mk_flamingo_gated_d2_seqx_r8_570098'

def setup_inputs(seed: int=0):
    np.random.seed(seed)
    _w = jnp.asarray

    def _rec_inputs():
        import jax
        import jax.numpy as jnp
        _rk = jax.random.key(seed)
        x = 0.000341 + 1 * jax.random.normal(jax.random.fold_in(_rk, 1), (16, 128, 256), jnp.float32)
        _lenS = 128 - jax.random.randint(jax.random.fold_in(_rk, 7), (16,), 0, max(1, 128 // 4) + 1, jnp.int32)
        _lenS2 = 128 - jax.random.randint(jax.random.fold_in(_rk, 8), (16,), 0, max(1, 128 // 4) + 1, jnp.int32)
        _ctx_2048P = jax.random.normal(jax.random.fold_in(_rk, 11), (16, 16, 256), jnp.float32)
        _ctx_2048c = jax.random.dirichlet(jax.random.fold_in(_rk, 511), 0.3 * jnp.ones((16,), jnp.float32), (16, 128))
        _ctx_2048t = jnp.einsum('bsk,bkd->bsd', _ctx_2048c, _ctx_2048P)
        _ctx_2048t = _ctx_2048t * jax.lax.rsqrt(jnp.mean(jnp.square(_ctx_2048t)) + 1e-12) * 0.953939
        ctx_2048 = -1.47943e-05 + 1.00017 * (_ctx_2048t + 0.3 * jax.random.normal(jax.random.fold_in(_rk, 611), (16, 128, 256), jnp.float32))
        _validS = jnp.arange(128)[None, :] < _lenS[:, None]
        _validS2 = jnp.arange(128)[None, :] < _lenS2[:, None]
        _causal = jnp.tril(jnp.ones((128, 128), dtype=bool))
        mask_BxS2_bk0 = jnp.logical_not(jnp.broadcast_to(_validS2[:, :], (16, 128)))
        _g = jax.random.normal(jax.random.fold_in(_rk, 9001), (2, 2), jnp.float32)
        _g = jnp.sign(_g) * jnp.maximum(jnp.abs(_g), 1.0) + (_g == 0) * 1.0
        g_xattn = _g[0]
        g_ffn = _g[1]
        return (x, ctx_2048, mask_BxS2_bk0, g_xattn, g_ffn)
    x, ctx_2048, mask_BxS2_bk0, g_xattn, g_ffn = _rec_inputs()

    def _L0_xattn_setup():
        import jax, jax.numpy as jnp
        import numpy as np

        def _wkv(time_decay, time_first, k, v):
            w = -jnp.exp(time_decay)
            u = time_first
            B, T, C = k.shape
            aa = jnp.zeros((B, C), dtype=k.dtype)
            bb = jnp.zeros((B, C), dtype=k.dtype)
            pp = jnp.full((B, C), -1e+38, dtype=k.dtype)

            def step(carry, kv_t):
                aa, bb, pp = carry
                kt, vt = kv_t
                ww = u + kt
                q = jnp.maximum(pp, ww)
                e1 = jnp.exp(pp - q)
                e2 = jnp.exp(ww - q)
                y_t = (e1 * aa + e2 * vt) / (e1 * bb + e2)
                ww2 = pp + w
                q2 = jnp.maximum(ww2, kt)
                e1b = jnp.exp(ww2 - q2)
                e2b = jnp.exp(kt - q2)
                new_carry = (e1b * aa + e2b * vt, e1b * bb + e2b, q2)
                return (new_carry, y_t)
            ks = jnp.transpose(k, (1, 0, 2))
            vs = jnp.transpose(v, (1, 0, 2))
            _, ys = jax.lax.scan(step, (aa, bb, pp), (ks, vs))
            return jnp.transpose(ys, (1, 0, 2))
        key = jax.random.key(seed)
        k1, k2, k3, k4 = jax.random.split(key, 4)
        B, T, C = (8, 128, 256)
        return {'batch_size': B, 'seq_len': T, 'embedding_dim': C, 'time_decay': jax.random.normal(k1, (C,), dtype=jnp.float32), 'time_first': jax.random.normal(k2, (C,), dtype=jnp.float32), 'k': jax.random.normal(k3, (B, T, C), dtype=jnp.float32), 'v': jax.random.normal(k4, (B, T, C), dtype=jnp.float32)}
    _L0_xattn_all = _L0_xattn_setup()
    _L0_xattn_in = {k: v for k, v in _L0_xattn_all.items() if k in ('time_decay', 'time_first')}
    del _L0_xattn_all

    def _L0_ffn_setup():
        import jax, jax.numpy as jnp
        import numpy as np
        HIDDEN = 256
        INTER = 1024
        SCALE = 64.0

        def fwht(x):
            orig_shape = x.shape
            n = orig_shape[-1]
            x = x.reshape(-1, n)
            h = 1
            while h < n:
                x = x.reshape(-1, n // (2 * h), 2, h)
                a, b = (x[:, :, 0, :], x[:, :, 1, :])
                x = jnp.stack([a + b, a - b], axis=2).reshape(-1, n)
                h *= 2
            return (x / jnp.sqrt(jnp.asarray(n, x.dtype))).reshape(orig_shape)
        key = jax.random.key(seed)
        ks = jax.random.split(key, 8)
        inp = jax.random.normal(ks[0], (4, 256, HIDDEN), dtype=jnp.float32)
        SU_ug = jnp.where(jax.random.bernoulli(ks[1], 0.5, (HIDDEN,)), 1.0, -1.0).astype(jnp.float32)
        SU_dp = jnp.where(jax.random.bernoulli(ks[2], 0.5, (INTER,)), 1.0, -1.0).astype(jnp.float32)
        Wscale_ug = jax.random.uniform(ks[3], (2 * INTER,), jnp.float32, 0.5, 1.5)
        Wscale_dp = jax.random.uniform(ks[4], (HIDDEN,), jnp.float32, 0.5, 1.5)
        W_up = jax.random.normal(ks[5], (INTER, HIDDEN), dtype=jnp.float32) * 0.02
        W_gate = jax.random.normal(ks[6], (INTER, HIDDEN), dtype=jnp.float32) * 0.02
        W_down = jax.random.normal(ks[7], (HIDDEN, INTER), dtype=jnp.float32) * 0.02
        return {'input': inp, 'SU_ug': SU_ug, 'SU_dp': SU_dp, 'Wscale_ug': Wscale_ug, 'Wscale_dp': Wscale_dp, 'W_up': W_up, 'W_gate': W_gate, 'W_down': W_down}
    _L0_ffn_all = _L0_ffn_setup()
    _L0_ffn_in = {k: v for k, v in _L0_ffn_all.items() if k in ('SU_ug', 'SU_dp', 'Wscale_ug', 'Wscale_dp', 'W_up', 'W_gate', 'W_down')}
    del _L0_ffn_all

    def _L1_xattn_setup():
        import jax, jax.numpy as jnp
        import numpy as np
        key = jax.random.key(seed)
        k1, k2, k3 = jax.random.split(key, 3)
        B, S, D, M = (8, 256, 256, 128)
        hidden_states = jax.random.normal(k1, (B, S, D), dtype=jnp.float32)
        memory_tokens = jax.random.normal(k2, (B, M, D), dtype=jnp.float32)
        memory_mask = jax.random.randint(k3, (B, M), 0, 2).astype(jnp.bool_)
        return {'hidden_states': hidden_states, 'memory_tokens': memory_tokens, 'memory_mask': memory_mask}
    _L1_xattn_all = _L1_xattn_setup()
    _L1_xattn_in = {k: v for k, v in _L1_xattn_all.items() if k in ()}
    del _L1_xattn_all

    def _L1_ffn_setup():
        import jax, jax.numpy as jnp
        import numpy as np
        B, S, D, R, E = (4, 256, 256, 64, 8)
        SCALING = 64.0 / 16.0
        key = jax.random.key(seed)
        k1, k2, k3, k4 = jax.random.split(key, 4)
        x = jax.random.normal(k1, (B, S, D), dtype=jnp.float32)
        A = jax.random.normal(k2, (E, R, D), dtype=jnp.float32) * 0.02
        Bw = jax.random.normal(k3, (E, D, R), dtype=jnp.float32) * 0.02
        Wg = jax.random.normal(k4, (E, D), dtype=jnp.float32) * 0.02
        return {'x': x, 'A': A, 'Bw': Bw, 'Wg': Wg}
    _L1_ffn_all = _L1_ffn_setup()
    _L1_ffn_in = {k: v for k, v in _L1_ffn_all.items() if k in ('A', 'Bw', 'Wg')}
    del _L1_ffn_all
    return {'x': x, 'ctx_2048': ctx_2048, 'mask_BxS2_bk0': mask_BxS2_bk0, 'g_xattn': g_xattn, 'g_ffn': g_ffn, 'L0_xattn_time_decay': _L0_xattn_in['time_decay'], 'L0_xattn_time_first': _L0_xattn_in['time_first'], 'L0_ffn_SU_ug': _L0_ffn_in['SU_ug'], 'L0_ffn_SU_dp': _L0_ffn_in['SU_dp'], 'L0_ffn_Wscale_ug': _L0_ffn_in['Wscale_ug'], 'L0_ffn_Wscale_dp': _L0_ffn_in['Wscale_dp'], 'L0_ffn_W_up': _L0_ffn_in['W_up'], 'L0_ffn_W_gate': _L0_ffn_in['W_gate'], 'L0_ffn_W_down': _L0_ffn_in['W_down'], 'L1_ffn_A': _L1_ffn_in['A'], 'L1_ffn_Bw': _L1_ffn_in['Bw'], 'L1_ffn_Wg': _L1_ffn_in['Wg']}

def reference(x, ctx_2048, mask_BxS2_bk0, g_xattn, g_ffn, L0_xattn_time_decay, L0_xattn_time_first, L0_ffn_SU_ug, L0_ffn_SU_dp, L0_ffn_Wscale_ug, L0_ffn_Wscale_dp, L0_ffn_W_up, L0_ffn_W_gate, L0_ffn_W_down, L1_ffn_A, L1_ffn_Bw, L1_ffn_Wg):
    import jax
    import jax.numpy as jnp

    def _L0_xattn_ref(batch_size, seq_len, embedding_dim, time_decay, time_first, k, v):
        import jax, jax.numpy as jnp
        import numpy as np

        def _wkv(time_decay, time_first, k, v):
            w = -jnp.exp(time_decay)
            u = time_first
            B, T, C = k.shape
            aa = jnp.zeros((B, C), dtype=k.dtype)
            bb = jnp.zeros((B, C), dtype=k.dtype)
            pp = jnp.full((B, C), -1e+38, dtype=k.dtype)

            def step(carry, kv_t):
                aa, bb, pp = carry
                kt, vt = kv_t
                ww = u + kt
                q = jnp.maximum(pp, ww)
                e1 = jnp.exp(pp - q)
                e2 = jnp.exp(ww - q)
                y_t = (e1 * aa + e2 * vt) / (e1 * bb + e2)
                ww2 = pp + w
                q2 = jnp.maximum(ww2, kt)
                e1b = jnp.exp(ww2 - q2)
                e2b = jnp.exp(kt - q2)
                new_carry = (e1b * aa + e2b * vt, e1b * bb + e2b, q2)
                return (new_carry, y_t)
            ks = jnp.transpose(k, (1, 0, 2))
            vs = jnp.transpose(v, (1, 0, 2))
            _, ys = jax.lax.scan(step, (aa, bb, pp), (ks, vs))
            return jnp.transpose(ys, (1, 0, 2))
        assert seq_len <= 128
        return _wkv(time_decay, time_first, k, v)

    def _L0_ffn_ref(input, SU_ug, SU_dp, Wscale_ug, Wscale_dp, W_up, W_gate, W_down):
        import jax, jax.numpy as jnp
        import numpy as np
        HIDDEN = 256
        INTER = 1024
        SCALE = 64.0

        def fwht(x):
            orig_shape = x.shape
            n = orig_shape[-1]
            x = x.reshape(-1, n)
            h = 1
            while h < n:
                x = x.reshape(-1, n // (2 * h), 2, h)
                a, b = (x[:, :, 0, :], x[:, :, 1, :])
                x = jnp.stack([a + b, a - b], axis=2).reshape(-1, n)
                h *= 2
            return (x / jnp.sqrt(jnp.asarray(n, x.dtype))).reshape(orig_shape)
        n = SU_ug.shape[0]
        x = input.reshape(-1, n)
        x = fwht(x * SU_ug) / SCALE
        x_up = x @ W_up.T * (Wscale_ug[:INTER] * SCALE)
        x_gate = x @ W_gate.T * (Wscale_ug[INTER:] * SCALE)
        x = jax.nn.silu(x_gate) * x_up
        x = fwht(x * SU_dp) / SCALE
        x = x @ W_down.T * (Wscale_dp * SCALE)
        return x.reshape(input.shape)

    def _L1_xattn_ref(hidden_states, memory_tokens, memory_mask):
        import jax, jax.numpy as jnp
        import numpy as np
        B, S, D = hidden_states.shape
        scale = 1.0 / jnp.sqrt(jnp.asarray(D, hidden_states.dtype))
        scores = jnp.einsum('bsd,bmd->bsm', hidden_states, memory_tokens) * scale
        neg_inf = jnp.asarray(-1e+30, scores.dtype)
        scores = jnp.where(memory_mask[:, None, :], scores, neg_inf)
        attn = jax.nn.softmax(scores, axis=-1)
        readout = jnp.einsum('bsm,bmd->bsd', attn, memory_tokens)
        valid_b = jnp.any(memory_mask, axis=-1)
        out = jnp.where(valid_b[:, None, None], readout, jnp.zeros_like(readout))
        return out

    def _L1_ffn_ref(x, A, Bw, Wg):
        import jax, jax.numpy as jnp
        import numpy as np
        B, S, D, R, E = (4, 256, 256, 64, 8)
        SCALING = 64.0 / 16.0
        bsz, seq_len, dim = x.shape
        xf = x.reshape(-1, dim)
        logits = jnp.einsum('nd,ed->ne', xf, Wg)
        prob = jax.nn.softmax(logits, axis=-1)
        gate = jnp.argmax(prob, axis=-1)
        prob_sel = jnp.take_along_axis(prob, gate[:, None], axis=1)
        mask = jax.nn.one_hot(gate, E, dtype=xf.dtype)
        h = jnp.einsum('nd,erd->ner', xf, A)
        h = h * mask[:, :, None]
        y = jnp.einsum('ner,eor->no', h, Bw)
        y = y * SCALING * prob_sel
        return y.reshape(bsz, seq_len, -1)
    x = x + jnp.tanh(g_xattn[0]) * _L0_xattn_ref(16, 128, 256, L0_xattn_time_decay, L0_xattn_time_first, _layernorm(x, axis=-1), ctx_2048)
    x = x + jnp.tanh(g_ffn[0]) * _L0_ffn_ref(_layernorm(x, axis=-1), L0_ffn_SU_ug, L0_ffn_SU_dp, L0_ffn_Wscale_ug, L0_ffn_Wscale_dp, L0_ffn_W_up, L0_ffn_W_gate, L0_ffn_W_down)
    x = x + jnp.tanh(g_xattn[1]) * _L1_xattn_ref(_layernorm(x, axis=-1), ctx_2048, mask_BxS2_bk0)
    x = x + jnp.tanh(g_ffn[1]) * _L1_ffn_ref(_layernorm(x, axis=-1), L1_ffn_A, L1_ffn_Bw, L1_ffn_Wg)
    return x

_drawn_inputs = setup_inputs


def setup_inputs(seed=0):
    import zlib

    import numpy as np

    out = dict(_drawn_inputs(seed))
    spreads = {'g_ffn': (-1.0, 0.6)}
    factors = {'L0_ffn_Wscale_ug': 5.717,
     'L0_ffn_Wscale_dp': 7.846,
     'L1_ffn_A': 8.0,
     'L1_ffn_Bw': 8.0,
     'L1_ffn_Wg': 8.0}
    for name, (base, spread) in spreads.items():
        noise = np.random.default_rng([zlib.crc32(name.encode()), seed]).standard_normal(out[name].shape)
        drawn = base * np.exp(spread * noise) if base else spread * noise
        out[name] = jnp.asarray(drawn.astype(out[name].dtype))
    for name, factor in factors.items():
        out[name] = (out[name] * factor).astype(out[name].dtype)
    return out
```

```python
import concourse.bass as bass
from concourse import mybir
from contextlib import ExitStack

B, T, D = 16, 128, 256
INTER = 1024
EXPERTS, RANK = 8, 64
P = 128
KH = D // P
GB = 2
GROUPS = B // GB
GW = GB * D
TW = GB * T
MI = INTER // P
ER = EXPERTS * RANK
ME = ER // P
PAIRS = MI // 2
LN_EPS = 1e-5
MASKED = -1e30 * D ** 0.5
SCALING = 4.0

C_TD, C_U, C_SUG, C_SUD, C_WSG, C_WSU, C_G, C_WDP = 0, 2, 4, 6, 14, 22, 30, 34
VECS = C_WDP + D

STEPS = dict(
    wkv_dve="stats0 stats1 aggr0 aggr1 var shift ev1 ev2 scan_b scan_a num rden y y0 x1 "
            "stats0n stats1n aggr0n aggr1n varn shiftn",
    wkv_pool="rstd den rstdn",
    wkv_act="norm0 norm1 e1_0 e1_1 e2_0 e2_1 norm0n norm1n",
    wkv_pe="nT yT",
    ffn_pe="nT gate0 up0 gate1 up1 gate2 up2 gate3 up3 down",
    ffn_act="nT tanh0 tanh1 tanh2 tanh3 tanh4 tanh5 tanh6 tanh7 norm0 norm1",
    ffn_dve="z0 h0 z1 h1 z2 h2 z3 h3 x2 stats0 stats1 aggr0 aggr1 var shift",
    ffn_pool="rstd",
    att_pe="nT scores pT pv",
    att_act="nT exp0 exp1 pT norm0 norm1",
    att_dve="rmax nbias valid rsum coef x3_0 x3_1 stats0 stats1 aggr0 aggr1 var shift",
    att_pool="rstd",
    moe_pe="nT logits h0 h1 ohT mask0 mask1 y",
    moe_act="nT exp ohT mask0 mask1",
    moe_dve="lmax diff ranked rtop onehot rsum rinv coef hm0 hm1 x4_0 x4_1",
)
STEPS = {k: v.split() for k, v in STEPS.items()}


def after(stage, step, g):
    return g * len(STEPS[stage]) + (STEPS[stage].index(step) + 1)


def flamingo_kernel(nc, x_tok, ctx_tok, ctx_chan, mask_row, vecs, w_up_t, w_gate_t, w_down_t,
                    a_t, b_t, wg_t, hadamard, ident_in, expand_in, rank_in, out_tok):
    fp32 = mybir.dt.float32
    bf16 = mybir.dt.bfloat16
    u8 = mybir.dt.uint8
    ALU = mybir.AluOpType
    ACT = mybir.ActivationFunctionType
    AX = mybir.AxisListType

    ctx = ExitStack()
    with ctx:
        def sb(name, shape, dt=fp32):
            return ctx.enter_context(nc.sbuf_tensor(name, shape, dt))

        def pb(name):
            return ctx.enter_context(nc.psum_tensor(name, [P, 512], fp32))

        x_all = sb("x_all", [P, GROUPS * GW])
        c_all = sb("c_all", [P, GROUPS * GW])
        v_all = sb("v_all", [P, GROUPS * KH * TW])

        vec = sb("vec", [P, VECS])
        had = sb("had", [P, 2 * P])
        ident = sb("ident", [P, P])
        ident_b = sb("ident_b", [P, P], bf16)
        raw_up = sb("raw_up", [P, KH, INTER])
        raw_gate = sb("raw_gate", [P, KH, INTER])
        raw_down = sb("raw_down", [P, MI, D])
        bfly = sb("bfly", [P, MI, D])
        w_up = sb("w_up", [P, KH, INTER])
        w_gate = sb("w_gate", [P, KH, INTER])
        w_down = sb("w_down", [P, MI, D])
        a_w = sb("a_w", [P, KH, ER])
        b_w = sb("b_w", [P, ME, D])
        wg_w = sb("wg_w", [P, KH, EXPERTS])
        expand_f = sb("expand_f", [EXPERTS, ER])
        expand = sb("expand", [EXPERTS, ER], bf16)
        rank = sb("rank", [P, GB * EXPERTS])
        mask_u = sb("mask_u", [1, B * T], u8)
        mask_b = sb("mask_b", [1, B * T])
        ones = sb("ones", [1, P])
        decay = sb("decay", [P, KH * TW])
        small = sb("small", [P, 40])
        expd, lam = small[:, 0:2], small[:, 2:4]
        neg_m, u_m = small[:, 4:6], small[:, 6:8]
        tg = small[:, 8:12]
        tg4 = small[:, 12:13]
        su16 = small[:, 14:16]
        hwsg = small[:, 16:24]
        frow = small[:, 24:32]
        wdp = sb("wdp", [P, D])
        neg_half = sb("neg_half", [P, GB])

        n1, n2, n3, n4 = (sb(f"n{k}", [P, GB, D]) for k in (1, 2, 3, 4))
        n2T, n3T, n4T = (sb(f"n{k}T", [P, KH, TW]) for k in (2, 3, 4))
        st = [sb(f"st{k}", [P, GB, 6]) for k in range(4)]
        mv = [sb(f"mv{k}", [P, GB, 2]) for k in range(4)]
        var = [sb(f"var{k}", [P, GB]) for k in range(4)]
        rstd = [sb(f"rstd{k}", [P, GB]) for k in range(4)]
        shift = [sb(f"shift{k}", [P, GB]) for k in range(4)]
        e1 = sb("e1", [P, KH * TW])
        e2 = sb("e2", [P, KH * TW])
        ev1 = sb("ev1", [P, KH * TW])
        ev2 = sb("ev2", [P, KH * TW])
        sum_b = sb("sum_b", [P, 1 + KH * TW])
        sum_a = sb("sum_a", [P, 1 + KH * TW])
        den = sb("den", [P, KH * TW])
        num = sb("num", [P, KH * TW])
        rden = sb("rden", [P, KH * TW])
        y_t = sb("y_t", [P, KH * TW])
        tanh_g = sb("tanh_g", [P, 2, 2 * TW])
        z_g = sb("z_g", [P, 2, 2 * TW])
        h_t = sb("h_t", [P, MI, TW])
        prob = sb("prob", [P, GB, T])
        probT = sb("probT", [P, GB, T])
        att = sb("att", [P, 16])
        rmax, nbias, valid = att[:, 0:2], att[:, 2:4], att[:, 4:6]
        psum_row, rsum, acoef = att[:, 6:8], att[:, 8:10], att[:, 10:12]
        moe = sb("moe", [P, 16])
        lmax, rtop, msum, mrinv, mcoef = (moe[:, 2 * k:2 * k + 2] for k in range(5))
        diff = sb("diff", [P, GB, EXPERTS])
        pexp = sb("pexp", [P, GB, EXPERTS])
        ranked = sb("ranked", [P, GB, EXPERTS])
        onehot = sb("onehot", [P, GB, EXPERTS], bf16)
        onehotT = sb("onehotT", [EXPERTS, GB, T], bf16)
        maskT = sb("maskT", [P, ME, TW], bf16)
        hm_t = sb("hm_t", [P, ME, TW])

        tp_a = pb("tp_a")
        tp_b = pb("tp_b")
        gate_p = [pb("gate_p0"), pb("gate_p1")]
        up_p = [pb("up_p0"), pb("up_p1")]
        down_p = pb("down_p")
        mix_p = pb("mix_p")

        def sem(name):
            return ctx.enter_context(nc.semaphore(name))

        S = {k: sem(k) for k in STEPS}
        first_in = sem("first_in")
        consts_in = sem("consts_in")
        up_in, gate_in, down_in = sem("up_in"), sem("gate_in"), sem("down_in")
        rest_in = sem("rest_in")
        small_in = sem("small_in")
        setup_act, setup_dve, setup_pool = sem("setup_act"), sem("setup_dve"), sem("setup_pool")
        prep_pe, prep_evac = sem("prep_pe"), sem("prep_evac")
        down_evac = sem("down_evac")
        stored = sem("stored")
        act_passed, dve_passed = sem("act_passed"), sem("dve_passed")

        block = ctx.enter_context(nc.Block())

        def pass_wait(eng, passed, g):
            if not isinstance(g, int):
                eng.sem_inc(passed, 1)

        def xg(g, b=None):
            if b is None:
                return x_all[:, bass.ds(g * GW, GW)]
            return x_all[:, bass.ds(g * GW + b * D, D)]

        def pipeline(eng, run):
            def flags(i):
                return dict(ffn=i < GROUPS, wkv=i + 1 < GROUPS, att=1 <= i <= GROUPS, last=i >= 2)
            for i in (0, 1):
                run(i, **flags(i))
            with eng.Fori(2, GROUPS - 1) as i:
                run(i, **flags(2))
            for i in range(GROUPS - 1, GROUPS + 2):
                run(i, **flags(i))

        @block.sync
        def _(sp):
            sp.dma_start(vec[:, :], vecs).then_inc(first_in, 16)
            sp.dma_start(x_all[:, 0:GW], x_tok[:, 0:GW]).then_inc(first_in, 16)
            sp.dma_start(ident[:, :], ident_in).then_inc(consts_in, 16)
            sp.dma_start(had[:, :], hadamard).then_inc(consts_in, 16)
            sp.dma_start(v_all[:, 0:GW], ctx_chan[:, 0:GW]).then_inc(first_in, 16)
            sp.dma_start(raw_up[:, :, :], w_up_t).then_inc(up_in, 16)
            sp.dma_start(raw_gate[:, :, :], w_gate_t).then_inc(gate_in, 16)
            sp.dma_start(raw_down[:, :, :], w_down_t).then_inc(down_in, 16)
            sp.dma_start(x_all[:, GW:], x_tok[:, GW:]).then_inc(rest_in, 16)
            sp.dma_start(v_all[:, GW:], ctx_chan[:, GW:]).then_inc(rest_in, 16)
            sp.dma_start(mask_u[:, :], mask_row).then_inc(small_in, 16)
            sp.dma_start(expand_f[:, :], expand_in).then_inc(small_in, 16)
            sp.dma_start(rank[:, :], rank_in).then_inc(small_in, 16)
            sp.dma_start(wg_w[:, :, :], wg_t).then_inc(small_in, 16)
            sp.dma_start(a_w[:, :, :], a_t).then_inc(small_in, 16)
            sp.dma_start(b_w[:, :, :], b_t).then_inc(small_in, 16)
            sp.dma_start(c_all[:, :], ctx_tok).then_inc(small_in, 16)

            def run(i, ffn, wkv, att, last):
                if last:
                    g = i - 2
                    sp.wait_ge(S["moe_dve"], after("moe_dve", "x4_1", g))
                    sp.dma_start(out_tok[:, bass.ds(g * GW, GW)], xg(g)).then_inc(stored, 16)
            pipeline(sp, run)
            sp.wait_ge(stored, 16 * GROUPS)

        @block.gpsimd
        def _(pool):
            pool.memset(neg_half[:, :], -0.5)
            pool.memset(ones[:, :], 1.0).then_inc(setup_pool, 1)

            def root(stage, src, k, g):
                pool.wait_ge(S[stage + "_dve"], after(stage + "_dve", src, g))
                nc.gpsimd.tensor_tensor(rstd[k][:, :], var[k][:, :], neg_half[:, :], ALU.pow)\
                    .then_inc(S[stage + "_pool"], 1)

            def wkv_part(g):
                pool.wait_ge(S["wkv_act"], after("wkv_act", "e2_1", g))
                pool.wait_ge(S["wkv_dve"], after("wkv_dve", "scan_b", g))
                nc.gpsimd.tensor_tensor(den[:, :], sum_b[:, 0:KH * TW], e2[:, :], ALU.add)\
                    .then_inc(S["wkv_pool"], 1)

            pool.wait_ge(setup_pool, 1)
            root("wkv", "var", 0, 0)
            pool.wait_ge(down_in, 16)
            for s, src, dst in ((1, raw_down, bfly), (2, bfly, raw_down)):
                a = src[:, :, :].rearrange("p (x s y) d -> p x s (y d)", s=2, y=s)
                o = dst[:, :, :].rearrange("p (x s y) d -> p x s (y d)", s=2, y=s)
                if s == 2:
                    pool.wait_ge(setup_pool, 3)
                nc.gpsimd.tensor_tensor(o[:, :, 0], a[:, :, 0], a[:, :, 1], ALU.add)\
                    .then_inc(setup_pool, 1)
                nc.gpsimd.tensor_tensor(o[:, :, 1], a[:, :, 0], a[:, :, 1], ALU.subtract)\
                    .then_inc(setup_pool, 1)
                if s == 1:
                    wkv_part(0)
                    root("wkv", "varn", 1, 0)
            pool.wait_ge(small_in, 16 * 7)
            nc.gpsimd.tensor_scalar(mask_b[:, :], mask_u[:, :], -1.0, -MASKED, ALU.add, ALU.mult)\
                .then_inc(setup_pool, 1)
            nc.gpsimd.tensor_copy(ident_b[:, :], ident[:, :]).then_inc(setup_pool, 1)
            nc.gpsimd.tensor_copy(expand[:, :], expand_f[:, :]).then_inc(setup_pool, 1)

            def run(i, ffn, wkv, att, last):
                if wkv:
                    root("wkv", "var", 0, i + 1)
                    wkv_part(i + 1)
                if att:
                    root("att", "var", 3, i - 1)
                if wkv:
                    root("wkv", "varn", 1, i + 1)
                if ffn:
                    root("ffn", "var", 2, i)
            pipeline(pool, run)

        @block.scalar
        def _(act):
            def norm(stage, names, k, src, dst, g):
                act.wait_ge(S[stage + "_dve"], after(stage + "_dve", names, g))
                pass_wait(act, act_passed, g)
                for b in range(GB):
                    nc.scalar.activation(dst[:, b, :], src(b), ACT.Identity,
                                         bias=shift[k][:, b:b + 1], scale=rstd[k][:, b:b + 1])\
                        .then_inc(S[stage + "_act"], 1)

            def wkv_exps(g):
                act.wait_ge(S["wkv_pe"], after("wkv_pe", "nT", g))
                if not (isinstance(g, int) and g == 0):
                    act.wait_ge(S["wkv_dve"], after("wkv_dve", "rden", g - 1))
                for dst, bias in ((e1, neg_m), (e2, u_m)):
                    for k in range(KH):
                        nc.scalar.activation(dst[:, k * TW:(k + 1) * TW], tp_a[:, k * TW:(k + 1) * TW],
                                             ACT.Exp, bias=bias[:, k:k + 1])\
                            .then_inc(S["wkv_act"], 1)

            act.wait_ge(first_in, 48)
            nc.scalar.activation(expd, vec[:, C_TD:C_TD + 2], ACT.Exp).then_inc(setup_act, 1)
            nc.scalar.activation(tg, vec[:, C_G:C_G + 4], ACT.Tanh).then_inc(setup_act, 1)
            act.wait_ge(setup_act, 1)
            nc.scalar.activation(lam, expd, ACT.Exp, scale=-1.0).then_inc(setup_act, 1)
            norm("wkv", "shift", 0, lambda b: xg(0, b), n1, 0)
            act.wait_ge(setup_dve, 1)
            wkv_exps(0)
            for n in range(8):
                dst = (w_up, w_gate)[n // 4]
                act.wait_ge(prep_pe, n + 1)
                nc.scalar.activation(dst[:, n // 2 % 2, n % 2 * 512:(n % 2 + 1) * 512],
                                     (gate_p + up_p)[n % 4][:, :], ACT.Copy,
                                     scale=su16[:, n // 2 % 2:n // 2 % 2 + 1]).then_inc(prep_evac, 1)
            norm("wkv", "shiftn", 1, lambda b: xg(0, b), n2, 0)

            def run(i, ffn, wkv, att, last):
                def copy(stage, src, dst, step):
                    nc.scalar.copy(dst, src).then_inc(S[stage + "_act"], 1)

                def tanh(p):
                    act.wait_ge(S["ffn_pe"], after("ffn_pe", f"gate{p}", i))
                    if p >= 2:
                        act.wait_ge(S["ffn_dve"], after("ffn_dve", f"z{p - 2}", i))
                    for m in (2 * p, 2 * p + 1):
                        c = slice(m % 2 * TW, (m % 2 + 1) * TW)
                        nc.scalar.activation(tanh_g[:, p % 2, c], gate_p[p % 2][:, c], ACT.Tanh,
                                             scale=hwsg[:, m:m + 1]).then_inc(S["ffn_act"], 1)

                if ffn:
                    act.wait_ge(S["ffn_pe"], after("ffn_pe", "nT", i))
                    copy("ffn", tp_a[:, :], n2T[:, :, :], "nT")
                    tanh(0)
                if wkv:
                    norm("wkv", "shift", 0, lambda b: xg(i + 1, b), n1, i + 1)
                if att:
                    act.wait_ge(S["att_pe"], after("att_pe", "nT", i - 1))
                    copy("att", tp_b[:, :], n3T[:, :, :], "nT")
                if ffn:
                    tanh(1)
                if att:
                    act.wait_ge(S["att_dve"], after("att_dve", "nbias", i - 1))
                    for b in range(GB):
                        nc.scalar.activation(prob[:, b, :], mix_p[:, b * T:(b + 1) * T], ACT.Exp,
                                             bias=nbias[:, b:b + 1], scale=D ** -0.5,
                                             accum_out=psum_row[:, b:b + 1])\
                            .then_inc(S["att_act"], 1)
                if wkv:
                    wkv_exps(i + 1)
                if ffn:
                    tanh(2)
                if att:
                    act.wait_ge(S["att_pe"], after("att_pe", "pT", i - 1))
                    copy("att", tp_b[:, 0:GB * T], probT[:, :, :], "pT")
                if ffn:
                    tanh(3)
                if att:
                    norm("att", "shift", 3, lambda b: xg(i - 1, b), n4, i - 1)
                    act.wait_ge(S["moe_pe"], after("moe_pe", "nT", i - 1))
                    copy("moe", tp_b[:, :], n4T[:, :, :], "nT")
                if wkv:
                    norm("wkv", "shiftn", 1, lambda b: xg(i + 1, b), n2, i + 1)
                if att:
                    act.wait_ge(S["moe_dve"], after("moe_dve", "diff", i - 1))
                    nc.scalar.activation(pexp[:, :, :], diff[:, :, :], ACT.Exp).then_inc(S["moe_act"], 1)
                    act.wait_ge(S["moe_pe"], after("moe_pe", "ohT", i - 1))
                    copy("moe", tp_b[0:EXPERTS, 0:GB * T // 2].bitcast(bf16), onehotT[:, :, :], "ohT")
                    for j in range(2):
                        act.wait_ge(S["moe_pe"], after("moe_pe", f"mask{j}", i - 1))
                        copy("moe", up_p[j][:, :], maskT[:, 2 * j:2 * j + 2, :], f"mask{j}")
                if ffn:
                    norm("ffn", "shift", 2, lambda b: xg(i, b), n3, i)
            pipeline(act, run)

        @block.vector
        def _(dve):
            def layernorm(stage, k, g, suffix=""):
                name, s = stage + "_dve", S[stage + "_dve"]
                pass_wait(dve, dve_passed, g)
                for b in range(GB):
                    nc.vector.bn_stats(st[k][:, b, :], xg(g, b)).then_inc(s, 1)
                dve.wait_ge(s, after(name, "stats1" + suffix, g))
                pass_wait(dve, dve_passed, g)
                for b in range(GB):
                    nc.vector.bn_aggr(mv[k][:, b, :], st[k][:, b, :]).then_inc(s, 1)
                dve.wait_ge(s, after(name, "aggr1" + suffix, g))
                nc.vector.tensor_scalar(var[k][:, :], mv[k][:, :, 1], LN_EPS, None, ALU.add).then_inc(s, 1)
                dve.wait_ge(S[stage + "_pool"], after(stage + "_pool", "rstd" + suffix, g))
                nc.vector.scalar_tensor_tensor(shift[k][:, :], mv[k][:, :, 0], -1.0, rstd[k][:, :],
                                               ALU.mult, ALU.mult).then_inc(s, 1)

            def wkv_sums(g):
                s, name = S["wkv_dve"], "wkv_dve"
                vg = v_all[:, bass.ds(g * KH * TW, KH * TW)]
                dve.wait_ge(S["wkv_act"], after("wkv_act", "e1_1", g))
                nc.vector.tensor_tensor(ev1[:, :], e1[:, :], vg, ALU.mult).then_inc(s, 1)
                dve.wait_ge(S["wkv_act"], after("wkv_act", "e2_1", g))
                nc.vector.tensor_tensor(ev2[:, :], e2[:, :], vg, ALU.mult).then_inc(s, 1)
                nc.vector.tensor_tensor_scan(sum_b[:, 1:], decay[:, :], e1[:, :], 0.0,
                                             ALU.mult, ALU.add).then_inc(s, 1)
                dve.wait_ge(s, after(name, "ev1", g))
                nc.vector.tensor_tensor_scan(sum_a[:, 1:], decay[:, :], ev1[:, :], 0.0,
                                             ALU.mult, ALU.add).then_inc(s, 1)
                dve.wait_ge(s, after(name, "scan_a", g))
                nc.vector.tensor_tensor(num[:, :], sum_a[:, 0:KH * TW], ev2[:, :], ALU.add).then_inc(s, 1)

            def wkv_quotient(g):
                s, name = S["wkv_dve"], "wkv_dve"
                vg = v_all[:, bass.ds(g * KH * TW, KH * TW)]
                dve.wait_ge(S["wkv_pool"], after("wkv_pool", "den", g))
                nc.vector.reciprocal(rden[:, :], den[:, :]).then_inc(s, 1)
                dve.wait_ge(s, after(name, "rden", g))
                nc.vector.tensor_tensor(y_t[:, :], num[:, :], rden[:, :], ALU.mult).then_inc(s, 1)
                dve.wait_ge(s, after(name, "y", g))
                pass_wait(dve, dve_passed, g)
                nc.vector.tensor_copy(y_t[:, :].rearrange("p (s t) -> p s t", t=T)[:, :, 0],
                                      vg.rearrange("p (s t) -> p s t", t=T)[:, :, 0]).then_inc(s, 1)

            def wkv_residual(g):
                s = S["wkv_dve"]
                dve.wait_ge(S["wkv_pe"], after("wkv_pe", "yT", g))
                dve.wait_ge(S["wkv_act"], after("wkv_act", "norm1", g))
                nc.vector.scalar_tensor_tensor(xg(g), tp_a[:, :], tg[:, 0:1], xg(g), ALU.mult, ALU.add)\
                    .then_inc(s, 1)
                dve.wait_ge(s, after("wkv_dve", "x1", g))
                layernorm("wkv", 1, g, "n")

            dve.wait_ge(first_in, 48)
            layernorm("wkv", 0, 0)
            nc.vector.memset(decay[:, :], 1.0)
            nc.vector.memset(sum_b[:, 0:1], 1.0)
            nc.vector.memset(sum_a[:, 0:1], 0.0)
            nc.vector.tensor_scalar(neg_m, vec[:, C_U:C_U + 2], 0.0, -1.0, ALU.max, ALU.mult)
            nc.vector.tensor_scalar(u_m, vec[:, C_U:C_U + 2], 0.0, None, ALU.min)
            nc.vector.tensor_scalar(su16, vec[:, C_SUG:C_SUG + 2], D ** -0.5, None, ALU.mult)
            nc.vector.tensor_scalar(hwsg, vec[:, C_WSG:C_WSG + 8], 0.5, None, ALU.mult).then_inc(setup_dve, 1)
            dve.wait_ge(setup_act, 3)
            dve.wait_ge(setup_dve, 1)
            for k in range(KH):
                nc.vector.tensor_scalar(decay[:, k * TW:(k + 1) * TW], decay[:, k * TW:(k + 1) * TW],
                                        lam[:, k:k + 1], None, ALU.mult).then_inc(setup_dve, 1)
            dve.wait_ge(setup_dve, 3)
            nc.vector.memset(decay[:, :].rearrange("p (s t) -> p s t", t=T)[:, :, 0], 0.0)\
                .then_inc(setup_dve, 1)
            nc.vector.tensor_tensor(frow, hwsg, vec[:, C_WSU:C_WSU + 8], ALU.mult).then_inc(setup_dve, 1)
            nc.vector.tensor_scalar(wdp[:, :], vec[:, C_WDP:C_WDP + D], tg[:, 2:3], INTER ** -0.5,
                                    ALU.mult, ALU.mult).then_inc(setup_dve, 1)
            nc.vector.tensor_scalar(tg4, tg[:, 3:4], SCALING, None, ALU.mult).then_inc(setup_dve, 1)
            dve.wait_ge(setup_dve, 7)
            nc.vector.tensor_tensor(frow, frow, vec[:, C_SUD:C_SUD + 8], ALU.mult).then_inc(setup_dve, 1)
            wkv_sums(0)
            wkv_quotient(0)
            wkv_residual(0)
            dve.wait_ge(setup_dve, 8)
            for j in range(4):
                dve.wait_ge(prep_pe, 8 + j + 1)
                for k in (j, j + 4):
                    nc.vector.scalar_tensor_tensor(w_down[:, k, :],
                                                   (gate_p + up_p)[j][:, k // 4 * D:(k // 4 + 1) * D],
                                                   frow[:, k:k + 1], wdp[:, :], ALU.mult, ALU.mult)\
                        .then_inc(down_evac, 1)
            dve.wait_ge(rest_in, 32)

            def run(i, ffn, wkv, att, last):
                def inner(p):
                    s = S["ffn_dve"]
                    dve.wait_ge(S["ffn_act"], after("ffn_act", f"tanh{2 * p + 1}", i))
                    nc.vector.scalar_tensor_tensor(z_g[:, p % 2, :], tanh_g[:, p % 2, :], 1.0, gate_p[p % 2][:, :],
                                                   ALU.add, ALU.mult).then_inc(s, 1)
                    dve.wait_ge(s, after("ffn_dve", f"z{p}", i))
                    dve.wait_ge(S["ffn_pe"], after("ffn_pe", f"up{p}", i))
                    nc.vector.tensor_tensor(h_t[:, 2 * p:2 * p + 2, :], z_g[:, p % 2, :].rearrange("p (m t) -> p m t", m=2),
                                            up_p[p % 2][:, :].rearrange("p (m t) -> p m t", m=2),
                                            ALU.mult).then_inc(s, 1)

                if wkv:
                    layernorm("wkv", 0, i + 1)
                if last:
                    g = i - 2
                    dve.wait_ge(S["moe_pe"], after("moe_pe", "y", g))
                    for b in range(GB):
                        nc.vector.scalar_tensor_tensor(xg(g, b), mix_p[:, b * D:(b + 1) * D],
                                                       mcoef[:, b:b + 1], xg(g, b), ALU.mult, ALU.add)\
                            .then_inc(S["moe_dve"], 1)
                if ffn:
                    inner(0)
                    inner(1)
                if att:
                    s, g = S["att_dve"], i - 1
                    dve.wait_ge(S["att_pe"], after("att_pe", "scores", g))
                    nc.vector.reduce_max(rmax, mix_p[:, 0:GB * T].rearrange("p (b t) -> p b t", b=GB),
                                         AX.X).then_inc(s, 1)
                    dve.wait_ge(s, after("att_dve", "rmax", g))
                    nc.vector.tensor_scalar(nbias, rmax, -(D ** -0.5), None, ALU.mult).then_inc(s, 1)
                    nc.vector.tensor_scalar(valid, rmax, MASKED / 2, tg[:, 1:2], ALU.is_gt, ALU.mult)\
                        .then_inc(s, 1)
                if wkv:
                    wkv_sums(i + 1)
                if ffn:
                    inner(2)
                if att:
                    dve.wait_ge(S["att_act"], after("att_act", "exp1", g))
                    nc.vector.reciprocal(rsum, psum_row).then_inc(s, 1)
                    dve.wait_ge(s, after("att_dve", "rsum", g))
                    nc.vector.tensor_tensor(acoef, rsum, valid, ALU.mult).then_inc(s, 1)
                if ffn:
                    inner(3)
                if att:
                    dve.wait_ge(S["att_pe"], after("att_pe", "pv", g))
                    dve.wait_ge(s, after("att_dve", "coef", g))
                    for b in range(GB):
                        nc.vector.scalar_tensor_tensor(xg(g, b), mix_p[:, b * D:(b + 1) * D],
                                                       acoef[:, b:b + 1], xg(g, b), ALU.mult, ALU.add)\
                            .then_inc(s, 1)
                    dve.wait_ge(s, after("att_dve", "x3_1", g))
                    layernorm("att", 3, g)
                if wkv:
                    wkv_quotient(i + 1)
                    wkv_residual(i + 1)
                if att:
                    s, g = S["moe_dve"], i - 1
                    lg = mix_p[:, 0:GB * EXPERTS].rearrange("p (b e) -> p b e", b=GB)
                    rk = rank[:, :].rearrange("p (b e) -> p b e", b=GB)
                    dve.wait_ge(S["moe_pe"], after("moe_pe", "logits", g))
                    nc.vector.reduce_max(lmax, lg, AX.X).then_inc(s, 1)
                    dve.wait_ge(s, after("moe_dve", "lmax", g))
                    nc.vector.tensor_tensor(diff[:, :, :], lg, lmax.unsqueeze(2).broadcast_to([P, GB, EXPERTS]),
                                            ALU.subtract).then_inc(s, 1)
                    dve.wait_ge(s, after("moe_dve", "diff", g))
                    nc.vector.scalar_tensor_tensor(ranked[:, :, :], diff[:, :, :], 0.0, rk,
                                                   ALU.is_ge, ALU.mult).then_inc(s, 1)
                    dve.wait_ge(s, after("moe_dve", "ranked", g))
                    nc.vector.reduce_max(rtop, ranked[:, :, :], AX.X).then_inc(s, 1)
                    dve.wait_ge(s, after("moe_dve", "rtop", g))
                    nc.vector.tensor_tensor(onehot[:, :, :], ranked[:, :, :],
                                            rtop.unsqueeze(2).broadcast_to([P, GB, EXPERTS]),
                                            ALU.is_equal).then_inc(s, 1)
                if ffn:
                    sf = S["ffn_dve"]
                    dve.wait_ge(S["ffn_pe"], after("ffn_pe", "down", i))
                    nc.vector.tensor_tensor(xg(i), down_p[:, :], xg(i), ALU.add).then_inc(sf, 1)
                    dve.wait_ge(sf, after("ffn_dve", "x2", i))
                    layernorm("ffn", 2, i)
                if att:
                    dve.wait_ge(S["moe_act"], after("moe_act", "exp", g))
                    nc.vector.reduce_sum(msum, pexp[:, :, :], AX.X).then_inc(s, 1)
                    dve.wait_ge(s, after("moe_dve", "rsum", g))
                    nc.vector.reciprocal(mrinv, msum).then_inc(s, 1)
                    dve.wait_ge(s, after("moe_dve", "rinv", g))
                    nc.vector.tensor_scalar(mcoef, mrinv, tg4, None, ALU.mult).then_inc(s, 1)
                    for j in range(2):
                        dve.wait_ge(S["moe_act"], after("moe_act", f"mask{j}", g))
                        nc.vector.tensor_tensor(hm_t[:, 2 * j:2 * j + 2, :],
                                                gate_p[j][:, :].rearrange("p (m t) -> p m t", m=2),
                                                maskT[:, 2 * j:2 * j + 2, :], ALU.mult).then_inc(s, 1)
            pipeline(dve, run)

        @block.tensor
        def _(pe):
            def to_channels(dst, src):
                for k in range(KH):
                    for b in range(GB):
                        c = k * TW + b * T
                        last = nc.tensor.transpose(dst[:, c:c + T], src[:, b, k * P:(k + 1) * P], ident[:, :])
                return last

            def y_to_tokens():
                for b in range(GB):
                    for k in range(KH):
                        last = nc.tensor.transpose(tp_a[:, b * D + k * P:b * D + (k + 1) * P],
                                                   y_t[:, k * TW + b * T:k * TW + (b + 1) * T], ident[:, :])
                return last

            pe.wait_ge(consts_in, 32)
            pe.wait_ge(S["wkv_act"], after("wkv_act", "norm1", 0))
            to_channels(tp_a, n1).then_inc(S["wkv_pe"], 1)
            for n in range(8):
                raw, half, c = (raw_up, raw_gate)[n // 4], n // 2 % 2, n % 2
                if n % 4 == 0:
                    pe.wait_ge((up_in, gate_in)[n // 4], 16)
                if n >= 4:
                    pe.wait_ge(prep_evac, n - 3)
                for k in range(KH):
                    sign = P if half and k else 0
                    last = nc.tensor.matmul((gate_p + up_p)[n % 4][:, :], had[:, sign:sign + P],
                                            raw[:, k, c * 512:(c + 1) * 512], start=k == 0, stop=k == 1)
                last.then_inc(prep_pe, 1)
            pe.wait_ge(S["wkv_act"], after("wkv_act", "e2_1", 0))
            pe.wait_ge(S["wkv_dve"], after("wkv_dve", "y0", 0))
            y_to_tokens().then_inc(S["wkv_pe"], 1)
            pe.wait_ge(setup_pool, 5)
            for j in range(4):
                pe.wait_ge(prep_evac, 4 + j + 1)
                for k in (j, j + 4):
                    for a in (j, j + 4):
                        sign = P if k >= 4 and a >= 4 else 0
                        last = nc.tensor.matmul((gate_p + up_p)[j][:, k // 4 * D:(k // 4 + 1) * D],
                                                had[:, sign:sign + P], raw_down[:, a, :],
                                                start=a == j, stop=a >= 4)
                last.then_inc(prep_pe, 1)
            pe.wait_ge(down_evac, 8)
            pe.wait_ge(setup_pool, 8)

            def run(i, ffn, wkv, att, last):
                def pair(p):
                    if p < 2:
                        if last:
                            pe.wait_ge(S["moe_dve"], after("moe_dve", f"hm{p}", i - 2))
                    else:
                        pe.wait_ge(S["ffn_dve"], after("ffn_dve", f"h{p - 2}", i))
                    for w, dst in ((w_gate, gate_p[p % 2]), (w_up, up_p[p % 2])):
                        for m in (2 * p, 2 * p + 1):
                            for k in range(KH):
                                o = nc.tensor.matmul(dst[:, m % 2 * TW:(m % 2 + 1) * TW],
                                                     w[:, k, m * P:(m + 1) * P], n2T[:, k, :],
                                                     start=k == 0, stop=k == KH - 1)
                        o.then_inc(S["ffn_pe"], 1)

                def down(b):
                    for m in range(MI):
                        o = nc.tensor.matmul(down_p[:, b * D:(b + 1) * D], h_t[:, m, b * T:(b + 1) * T],
                                             w_down[:, m, :], start=m == 0, stop=m == MI - 1)
                    return o

                g = i - 1
                if ffn:
                    pe.wait_ge(S["wkv_act"], after("wkv_act", "norm1n", i))
                    to_channels(tp_a, n2).then_inc(S["ffn_pe"], 1)
                if last:
                    pe.wait_ge(S["moe_dve"], after("moe_dve", "hm1", i - 2))
                    for b in range(GB):
                        for m in range(ME):
                            o = nc.tensor.matmul(mix_p[:, b * D:(b + 1) * D], hm_t[:, m, b * T:(b + 1) * T],
                                                 b_w[:, m, :], start=m == 0, stop=m == ME - 1)
                    o.then_inc(S["moe_pe"], 1)
                if ffn:
                    pe.wait_ge(S["ffn_act"], after("ffn_act", "nT", i))
                    pair(0)
                if att:
                    pe.wait_ge(S["ffn_act"], after("ffn_act", "norm1", g))
                    to_channels(tp_b, n3).then_inc(S["att_pe"], 1)
                if ffn:
                    pair(1)
                if att:
                    pe.wait_ge(S["att_act"], after("att_act", "nT", g))
                    if last:
                        pe.wait_ge(S["moe_dve"], after("moe_dve", "x4_1", i - 2))
                    for b in range(GB):
                        for k in range(KH):
                            nc.tensor.matmul(mix_p[:, b * T:(b + 1) * T], n3T[:, k, b * T:(b + 1) * T],
                                             v_all[:, bass.ds(g * GW + k * TW + b * T, T)],
                                             start=k == 0, stop=False)
                        o = nc.tensor.matmul(mix_p[:, b * T:(b + 1) * T], ones[:, :],
                                             mask_b[:, bass.ds(g * TW + b * T, T)],
                                             start=False, stop=True)
                    o.then_inc(S["att_pe"], 1)
                if wkv:
                    pe.wait_ge(S["wkv_act"], after("wkv_act", "norm1", i + 1))
                    to_channels(tp_a, n1).then_inc(S["wkv_pe"], 1)
                if ffn:
                    pair(2)
                if att:
                    pe.wait_ge(S["att_act"], after("att_act", "exp1", g))
                    for b in range(GB):
                        o = nc.tensor.transpose(tp_b[:, b * T:(b + 1) * T], prob[:, b, :], ident[:, :])
                    o.then_inc(S["att_pe"], 1)
                if ffn:
                    pair(3)
                if att:
                    pe.wait_ge(S["att_act"], after("att_act", "pT", g))
                    for b in range(GB):
                        o = nc.tensor.matmul(mix_p[:, b * D:(b + 1) * D], probT[:, b, :],
                                             c_all[:, bass.ds(g * GW + b * D, D)], start=True, stop=True)
                    o.then_inc(S["att_pe"], 1)
                if ffn:
                    pe.wait_ge(S["ffn_dve"], after("ffn_dve", "h3", i))
                    down(0)
                if att:
                    pe.wait_ge(S["att_act"], after("att_act", "norm1", g))
                    to_channels(tp_b, n4).then_inc(S["moe_pe"], 1)
                if ffn:
                    down(1).then_inc(S["ffn_pe"], 1)
                if wkv:
                    pe.wait_ge(S["wkv_dve"], after("wkv_dve", "y0", i + 1))
                    y_to_tokens().then_inc(S["wkv_pe"], 1)
                if att:
                    pe.wait_ge(S["moe_act"], after("moe_act", "nT", g))
                    for b in range(GB):
                        for k in range(KH):
                            o = nc.tensor.matmul(mix_p[:, b * EXPERTS:(b + 1) * EXPERTS],
                                                 n4T[:, k, b * T:(b + 1) * T], wg_w[:, k, :],
                                                 start=k == 0, stop=k == KH - 1)
                    o.then_inc(S["moe_pe"], 1)
                    for m in range(ME):
                        for k in range(KH):
                            o = nc.tensor.matmul(gate_p[m // 2][:, m % 2 * TW:(m % 2 + 1) * TW],
                                                 a_w[:, k, m * P:(m + 1) * P], n4T[:, k, :],
                                                 start=k == 0, stop=k == KH - 1)
                        if m % 2:
                            o.then_inc(S["moe_pe"], 1)
                    pe.wait_ge(S["moe_dve"], after("moe_dve", "onehot", g))
                    for b in range(GB):
                        o = nc.tensor.transpose(tp_b[0:EXPERTS, b * T // 2:(b + 1) * T // 2].bitcast(bf16),
                                                onehot[:, b, :], ident_b[:, :])
                    o.then_inc(S["moe_pe"], 1)
                    pe.wait_ge(S["moe_act"], after("moe_act", "ohT", g))
                    for m in range(ME):
                        o = nc.tensor.matmul(up_p[m // 2][:, m % 2 * TW:(m % 2 + 1) * TW],
                                             expand[:, m * P:(m + 1) * P], onehotT[:, :, :],
                                             start=True, stop=True)
                        if m % 2:
                            o.then_inc(S["moe_pe"], 1)
            pipeline(pe, run)


def kernel(x, ctx_2048, mask_BxS2_bk0, g_xattn, g_ffn, L0_xattn_time_decay, L0_xattn_time_first,
           L0_ffn_SU_ug, L0_ffn_SU_dp, L0_ffn_Wscale_ug, L0_ffn_Wscale_dp, L0_ffn_W_up,
           L0_ffn_W_gate, L0_ffn_W_down, L1_ffn_A, L1_ffn_Bw, L1_ffn_Wg):
    import numpy as np
    import concourse.bacc as bacc
    from concourse.bass_utils import run_bass_kernel_spmd

    c = np.ascontiguousarray

    def chunks(a):
        return c(a.reshape(a.shape[0] // P, P, a.shape[1]).transpose(1, 0, 2))

    def cols(v):
        return np.asarray(v).reshape(-1, P).T

    x, ctx = np.asarray(x), np.asarray(ctx_2048)
    gates = np.concatenate([np.asarray(g_xattn), np.asarray(g_ffn)])
    wug = np.asarray(L0_ffn_Wscale_ug)
    vecs = np.concatenate([
        cols(L0_xattn_time_decay), cols(L0_xattn_time_first), cols(L0_ffn_SU_ug), cols(L0_ffn_SU_dp),
        cols(wug[INTER:]), cols(wug[:INTER]), np.broadcast_to(gates, (P, 4)),
        np.broadcast_to(np.asarray(L0_ffn_Wscale_dp), (P, D))], axis=1)
    had = np.ones((1, 1), np.float32)
    while had.shape[0] < P:
        had = np.block([[had, had], [had, -had]])
    arrays = {
        "x_tok": c(x.transpose(1, 0, 2)).reshape(P, B * D),
        "ctx_tok": c(ctx.transpose(1, 0, 2)).reshape(P, B * D),
        "ctx_chan": c(ctx.reshape(GROUPS, GB, T, KH, P).transpose(4, 0, 3, 1, 2)).reshape(P, -1),
        "mask_row": np.asarray(mask_BxS2_bk0).reshape(1, B * T),
        "vecs": c(vecs),
        "w_up_t": chunks(np.asarray(L0_ffn_W_up).T),
        "w_gate_t": chunks(np.asarray(L0_ffn_W_gate).T),
        "w_down_t": chunks(np.asarray(L0_ffn_W_down).T),
        "a_t": chunks(np.asarray(L1_ffn_A).reshape(ER, D).T),
        "b_t": chunks(np.asarray(L1_ffn_Bw).transpose(0, 2, 1).reshape(ER, D)),
        "wg_t": chunks(np.asarray(L1_ffn_Wg).T),
        "hadamard": np.concatenate([had, -had], axis=1).astype(np.float32),
        "ident_in": np.eye(P, dtype=np.float32),
        "expand_in": np.repeat(np.eye(EXPERTS, dtype=np.float32), RANK, axis=1),
        "rank_in": np.broadcast_to(np.arange(EXPERTS, 0, -1, dtype=np.float32), (P, GB, EXPERTS)).reshape(P, -1).copy(),
    }
    nc = bacc.Bacc("TRN2", target_bir_lowering=False, num_devices=1)
    args = [nc.dram_tensor(n, a.shape, mybir.dt.from_np(a.dtype), kind="ExternalInput").ap()
            for n, a in arrays.items()]
    out = nc.dram_tensor("out_tok", (P, B * D), mybir.dt.float32, kind="ExternalOutput").ap()
    flamingo_kernel(nc, *args, out)
    r = run_bass_kernel_spmd(nc, [arrays], core_ids=[0])
    got = r.results[0]["out_tok"]
    return c(np.asarray(got).reshape(T, B, D).transpose(1, 0, 2))
```

```python
import concourse.bass as bass
from concourse import mybir
from contextlib import ExitStack

B, T, D = 16, 128, 256
INTER = 1024
EXPERTS, RANK = 8, 64
P = 128
KH = D // P
GB = 2
GROUPS = B // GB
GW = GB * D
TW = GB * T
MI = INTER // P
ER = EXPERTS * RANK
ME = ER // P
PAIRS = MI // 2
LN_EPS = 1e-5
MASKED = -1e30 * D ** 0.5
SCALING = 4.0
PREP = 4 * KH

N_SCALE = 2.0 ** 6
W_SCALE = 2.0 ** 6
H_SCALE = 2.0 ** -26
A_SCALE = 2.0 ** 8
M_SCALE = 2.0 ** -7
L_SCALE = 2.0 ** 14
DOWN_STEPS = [(a, m) for a in range(2) for m in range(MI)]
TINY = 1e-30

C_TD, C_U, C_SUG, C_SUD, C_WSG, C_WSU, C_G, C_WDP = 0, 2, 4, 6, 14, 22, 30, 34
VECS = C_WDP + D

STEPS = dict(
    wkv_dve="stats0 stats1 aggr0 aggr1 var shift scan_b ev1 den scan_a y0 rden0 rden1 y x1 "
            "stats0n stats1n aggr0n aggr1n varn shiftn",
    wkv_pool="rstd ev2 num rstdn",
    wkv_act="norm0 norm1 e1_0 e1_1 e2_0 e2_1 norm0n norm1n",
    wkv_pe="nT yT",
    ffn_pe="nT gate0 up0 gate1 up1 gate2 up2 gate3 up3 down",
    ffn_act="hi tanh0 tanh1 tanh2 tanh3 hhi0 hhi1 tanh4 tanh5 tanh6 tanh7 hhi2 hhi3",
    ffn_dve="lo z0 h0 z1 h1 z2 h2 z3 h3 x2",
    ffn_pool="hlo0 hlo1 hlo2 hlo3",
    att_pe="nT scores pT pv",
    att_act="norm0 norm1 nT exp0 exp1 pT norm0n norm1n",
    att_dve="stats0 stats1 aggr0 aggr1 var shift rmax nbias valid rsum coef x3_0 x3_1 "
            "stats0n stats1n aggr0n aggr1n varn shiftn",
    att_pool="rstd rstdn",
    moe_pe="nT logits h0 h1 ohT mask0 mask1",
    moe_act="hi exp hc0 hc1 ohT mhi0 mhi1",
    moe_dve="lo lmax diff ranked rtop onehot rsum rinv coef hm0 hm1",
    moe_pool="mlo0 mlo1",
    out_pe="y",
    out_dve="x4_0 x4_1",
)
STEPS = {k: v.split() for k, v in STEPS.items()}


def after(stage, step, g):
    return g * len(STEPS[stage]) + (STEPS[stage].index(step) + 1)


def flamingo_kernel(nc, x_tok, ctx_tok, ctx_chan, mask_row, vecs, w_up_t, w_gate_t, w_down_t,
                    a_t, b_t, wg_t, hadamard, ident_in, expand_in, rank_in, out_tok):
    fp32 = mybir.dt.float32
    bf16 = mybir.dt.bfloat16
    f16 = mybir.dt.float16
    u8 = mybir.dt.uint8
    ALU = mybir.AluOpType
    ACT = mybir.ActivationFunctionType
    AX = mybir.AxisListType

    ctx = ExitStack()
    with ctx:
        def sb(name, shape, dt=fp32):
            return ctx.enter_context(nc.sbuf_tensor(name, shape, dt))

        def pb(name):
            return ctx.enter_context(nc.psum_tensor(name, [P, 512], fp32))

        x_all = sb("x_all", [P, GROUPS * GW])
        c_all = sb("c_all", [P, GROUPS * GW])
        v_all = sb("v_all", [P, GROUPS * KH * TW])

        vec = sb("vec", [P, VECS])
        had = sb("had", [P, 2 * P])
        ident = sb("ident", [P, P])
        ident_b = sb("ident_b", [P, P], bf16)
        raw_up = sb("raw_up", [P, KH, INTER])
        raw_gate = sb("raw_gate", [P, KH, INTER])
        raw_down = sb("raw_down", [P, MI, D])
        bfly = sb("bfly", [P, MI, D])
        w_down = raw_up[:, :, :].rearrange("p k (m d) -> p (k m) d", d=D)
        a_w = sb("a_w", [P, KH, ER])
        b_w = sb("b_w", [P, ME, D])
        wg_w = sb("wg_w", [P, KH, EXPERTS])
        up_h = [sb(f"up_h{k}", [P, KH, INTER], f16) for k in range(2)]
        gate_h = [sb(f"gate_h{k}", [P, KH, INTER], f16) for k in range(2)]
        down_h = [sb(f"down_h{k}", [P, MI, D], f16) for k in range(2)]
        a_h = [sb(f"a_h{k}", [P, KH, ER], f16) for k in range(2)]
        b_h = [sb(f"b_h{k}", [P, ME, D], f16) for k in range(2)]
        wg_h = [sb(f"wg_h{k}", [P, KH, EXPERTS], f16) for k in range(2)]
        expand_f = sb("expand_f", [EXPERTS, ER])
        expand = sb("expand", [EXPERTS, ER], bf16)
        rank = sb("rank", [P, GB * EXPERTS])
        mask_u = sb("mask_u", [1, B * T], u8)
        mask_b = sb("mask_b", [1, B * T])
        ones = sb("ones", [1, P])
        decay = sb("decay", [P, KH * TW])
        small = sb("small", [P, 40])
        expd, lam = small[:, 0:2], small[:, 2:4]
        neg_m, u_m = small[:, 4:6], small[:, 6:8]
        tg = small[:, 8:12]
        tg4 = small[:, 12:13]
        hwsg = small[:, 16:24]
        frow = small[:, 24:32]
        amax = sb("amax", [P, 6])
        gmax = sb("gmax", [P, 6])
        ginv = sb("ginv", [P, 6])
        sus = sb("sus", [P, 2, KH])
        wsc = sb("wsc", [P, 4])
        unsc = sb("unsc", [P, 3])
        wdp = sb("wdp", [P, D])
        neg_half = sb("neg_half", [P, GB])

        n1, n2, n3, n4 = (sb(f"n{k}", [P, GB, D]) for k in (1, 2, 3, 4))
        n3T = sb("n3T", [P, KH, TW])
        n2h, n4h = ([sb(f"n{k}h{j}", [P, KH, TW], f16) for j in range(2)] for k in (2, 4))
        st = [sb(f"st{k}", [P, GB, 6]) for k in range(4)]
        mv = [sb(f"mv{k}", [P, GB, 2]) for k in range(4)]
        var = [sb(f"var{k}", [P, GB]) for k in range(4)]
        rstd = [sb(f"rstd{k}", [P, GB]) for k in range(4)]
        shift = [sb(f"shift{k}", [P, GB]) for k in range(4)]
        e1 = sb("e1", [P, KH * TW])
        e2 = sb("e2", [P, KH * TW])
        ev1 = sb("ev1", [P, KH * TW])
        ev2 = sb("ev2", [P, KH * TW])
        sum_b = sb("sum_b", [P, 1 + KH * TW])
        sum_a = sb("sum_a", [P, 1 + KH * TW])
        den = sb("den", [P, KH * TW])
        num = sb("num", [P, KH * TW])
        rden = sb("rden", [P, KH * TW])
        y_t = sb("y_t", [P, KH * TW])
        tanh_g = sb("tanh_g", [P, 2, 2 * TW])
        z_g = sb("z_g", [P, 2, 2 * TW])
        h_f = sb("h_f", [P, 2, 2 * TW])
        h_h = [sb(f"h_h{k}", [P, MI, TW], f16) for k in range(2)]
        prob = sb("prob", [P, GB, T])
        probT = sb("probT", [P, GB, T])
        att = sb("att", [P, 16])
        rmax, nbias, valid = att[:, 0:2], att[:, 2:4], att[:, 4:6]
        psum_row, rsum, acoef = att[:, 6:8], att[:, 8:10], att[:, 10:12]
        moe = sb("moe", [P, 16])
        lmax, rtop, msum, mrinv, mcoef = (moe[:, 2 * k:2 * k + 2] for k in range(5))
        diff = sb("diff", [P, GB, EXPERTS])
        pexp = sb("pexp", [P, GB, EXPERTS])
        ranked = sb("ranked", [P, GB, EXPERTS])
        onehot = sb("onehot", [P, GB, EXPERTS], bf16)
        onehotT = sb("onehotT", [EXPERTS, GB, T], bf16)
        hc, hm_f = (raw_gate[:, k, :].rearrange("p (m t) -> p m t", t=TW) for k in range(2))
        hm_h = [sb(f"hm_h{k}", [P, ME, TW], f16) for k in range(2)]

        tp_a = pb("tp_a")
        tp_b = pb("tp_b")
        gate_p = [pb("gate_p0"), pb("gate_p1")]
        up_p = [pb("up_p0"), pb("up_p1")]
        down_p = pb("down_p")
        mix_p = pb("mix_p")

        def sem(name):
            return ctx.enter_context(nc.semaphore(name))

        S = {k: sem(k) for k in STEPS}
        x0_in, vec_in, v0_in = sem("x0_in"), sem("vec_in"), sem("v0_in")
        consts_in = sem("consts_in")
        up_in, gate_in, down_in = sem("up_in"), sem("gate_in"), sem("down_in")
        rest_in = sem("rest_in")
        small_in = sem("small_in")
        ctx_in = sem("ctx_in")
        setup_act, setup_dve, setup_pool = sem("setup_act"), sem("setup_dve"), sem("setup_pool")
        prep_pe, prep_evac = sem("prep_pe"), sem("prep_evac")
        prep_lo = sem("prep_lo")
        up_max, gate_max, down_max, moe_max = (sem(f"{k}_max") for k in ("up", "gate", "down", "moe"))
        up_all, gate_all, down_all, moe_all = (sem(f"{k}_all") for k in ("up", "gate", "down", "moe"))
        ug_scaled, down_scaled, moe_scaled = (sem(f"{k}_scaled") for k in ("ug", "down", "moe"))
        prep_down, down_f32 = sem("prep_down"), sem("down_f32")
        down_hi, down_lo, moe_hi, moe_lo = (sem(k) for k in ("down_hi", "down_lo", "moe_hi", "moe_lo"))
        bfly_done, small_ready = sem("bfly_done"), sem("small_ready")
        stored = sem("stored")
        scale_steps = sem("scale_steps")
        act_passed, dve_passed, pool_passed = sem("act_passed"), sem("dve_passed"), sem("pool_passed")

        block = ctx.enter_context(nc.Block())

        def pass_wait(eng, passed, g):
            if not isinstance(g, int):
                eng.sem_inc(passed, 1)

        def xg(g, b=None):
            if b is None:
                return x_all[:, bass.ds(g * GW, GW)]
            return x_all[:, bass.ds(g * GW + b * D, D)]

        prep_bank = [gate_p[0], gate_p[1], up_p[0], up_p[1], down_p, mix_p, tp_b, gate_p[1]]
        down_bank = [tp_b, mix_p, down_p, tp_b]
        by_arrival = [0, 1, 4, 5, 2, 3, 6, 7]

        def chunk(n):
            return n // 2 % 2, n % 2, n // 4

        def arrived(n):
            return by_arrival.index(n) + 1

        def pipeline(eng, run):
            def flags(i):
                return dict(ffn=i < GROUPS, wkv=i + 1 < GROUPS, att=1 <= i <= GROUPS, last=i >= 2)
            for i in (0, 1):
                run(i, **flags(i))
            with eng.Fori(2, GROUPS - 1) as i:
                run(i, **flags(2))
            for i in range(GROUPS - 1, GROUPS + 2):
                run(i, **flags(i))

        @block.sync
        def _(sp):
            sp.dma_start(x_all[:, 0:GW], x_tok[:, 0:GW]).then_inc(x0_in, 16)
            sp.dma_start(vec[:, :], vecs).then_inc(vec_in, 16)
            sp.dma_start(ident[:, :], ident_in).then_inc(consts_in, 16)
            sp.dma_start(v_all[:, 0:GW], ctx_chan[:, 0:GW]).then_inc(v0_in, 16)
            sp.dma_start(had[:, :], hadamard).then_inc(consts_in, 16)
            sp.dma_start(raw_up[:, :, :], w_up_t).then_inc(up_in, 16)
            sp.dma_start(raw_gate[:, :, :], w_gate_t).then_inc(gate_in, 16)
            sp.dma_start(raw_down[:, :, :], w_down_t).then_inc(down_in, 16)
            sp.dma_start(x_all[:, GW:], x_tok[:, GW:]).then_inc(rest_in, 16)
            sp.dma_start(v_all[:, GW:], ctx_chan[:, GW:]).then_inc(rest_in, 16)
            sp.dma_start(mask_u[:, :], mask_row).then_inc(small_in, 16)
            sp.dma_start(expand_f[:, :], expand_in).then_inc(small_in, 16)
            sp.dma_start(rank[:, :], rank_in).then_inc(small_in, 16)
            sp.dma_start(a_w[:, :, :], a_t).then_inc(small_in, 16)
            sp.dma_start(b_w[:, :, :], b_t).then_inc(small_in, 16)
            sp.dma_start(wg_w[:, :, :], wg_t).then_inc(small_in, 16)
            sp.dma_start(c_all[:, :], ctx_tok).then_inc(ctx_in, 16)

            def run(i, ffn, wkv, att, last):
                if last:
                    g = i - 2
                    sp.wait_ge(S["out_dve"], after("out_dve", "x4_1", g))
                    sp.dma_start(out_tok[:, bass.ds(g * GW, GW)], xg(g)).then_inc(stored, 16)
            pipeline(sp, run)
            sp.wait_ge(stored, 16 * GROUPS)

        @block.gpsimd
        def _(pool):
            pool.memset(neg_half[:, :], -0.5)
            pool.memset(ones[:, :], 1.0).then_inc(setup_pool, 1)

            def root(stage, src, k, g):
                pool.wait_ge(S[stage + "_dve"], after(stage + "_dve", src, g))
                nc.gpsimd.tensor_tensor(rstd[k][:, :], var[k][:, :], neg_half[:, :], ALU.pow)\
                    .then_inc(S[stage + "_pool"], 1)

            def wkv_weighted(g):
                pool.wait_ge(S["wkv_act"], after("wkv_act", "e2_1", g))
                pass_wait(pool, pool_passed, g)
                nc.gpsimd.tensor_tensor(ev2[:, :], e2[:, :], v_all[:, bass.ds(g * KH * TW, KH * TW)],
                                        ALU.mult).then_inc(S["wkv_pool"], 1)

            def wkv_numerator(g):
                pool.wait_ge(S["wkv_dve"], after("wkv_dve", "scan_a", g))
                pool.wait_ge(S["wkv_pool"], after("wkv_pool", "ev2", g))
                nc.gpsimd.tensor_tensor(num[:, :], sum_a[:, 0:KH * TW], ev2[:, :], ALU.add)\
                    .then_inc(S["wkv_pool"], 1)

            def all_max(cols, ready, done):
                pool.wait_ge(ready, cols.stop - cols.start)
                nc.gpsimd.partition_all_reduce(gmax[:, cols], amax[:, cols], P, bass.bass_isa.ReduceOp.max)\
                    .then_inc(done, 1)

            def butterfly(s, half):
                src, dst = ((raw_down, bfly), (bfly, raw_down))[s % 4 // 2]
                a = src[:, :, :].rearrange("p (x s y) d -> p x s (y d)", s=2, y=s)
                o = dst[:, :, :].rearrange("p (x s y) d -> p x s (y d)", s=2, y=s)
                nc.gpsimd.tensor_tensor(o[:, :, half], a[:, :, 0], a[:, :, 1],
                                        (ALU.add, ALU.subtract)[half]).then_inc(bfly_done, 1)

            pool.wait_ge(setup_pool, 1)
            root("wkv", "var", 0, 0)
            all_max(slice(0, 1), up_max, up_all)
            pool.wait_ge(v0_in, 16)
            wkv_weighted(0)
            wkv_numerator(0)
            pool.wait_ge(down_in, 16)
            butterfly(1, 0)
            all_max(slice(1, 2), gate_max, gate_all)
            root("wkv", "varn", 1, 0)
            butterfly(1, 1)
            pool.wait_ge(bfly_done, 2)
            butterfly(2, 0)
            butterfly(2, 1)

            def setup_small():
                pool.wait_ge(small_in, 16 * 6)
                nc.gpsimd.tensor_scalar(mask_b[:, :], mask_u[:, :], -1.0, -MASKED, ALU.add, ALU.mult)\
                    .then_inc(small_ready, 1)
                nc.gpsimd.tensor_copy(ident_b[:, :], ident[:, :]).then_inc(small_ready, 1)
                nc.gpsimd.tensor_copy(expand[:, :], expand_f[:, :]).then_inc(small_ready, 1)

            def run(i, ffn, wkv, att, last):
                def low(p):
                    pool.wait_ge(S["ffn_act"], after("ffn_act", f"hhi{p}", i))
                    nc.gpsimd.tensor_tensor(h_h[1][:, 2 * p:2 * p + 2, :],
                                            h_f[:, p % 2, :].rearrange("p (m t) -> p m t", m=2),
                                            h_h[0][:, 2 * p:2 * p + 2, :], ALU.subtract)\
                        .then_inc(S["ffn_pool"], 1)

                first, second = (isinstance(i, int) and i == n for n in (0, 1))
                if wkv:
                    root("wkv", "var", 0, i + 1)
                if att:
                    root("att", "var", 2, i - 1)
                def mask_low(j):
                    pool.wait_ge(S["moe_act"], after("moe_act", f"mhi{j}", i - 2))
                    nc.gpsimd.tensor_tensor(hm_h[1][:, 2 * j:2 * j + 2, :], hm_f[:, 2 * j:2 * j + 2, :],
                                            hm_h[0][:, 2 * j:2 * j + 2, :], ALU.subtract)\
                        .then_inc(S["moe_pool"], 1)

                if first:
                    pool.wait_ge(bfly_done, 4)
                    butterfly(4, 0)
                    butterfly(4, 1)
                    setup_small()
                    pool.wait_ge(rest_in, 32)
                if ffn:
                    low(0)
                if wkv:
                    wkv_weighted(i + 1)
                if ffn:
                    low(1)
                if wkv and not first:
                    wkv_numerator(i + 1)
                if first:
                    all_max(slice(2, 3), down_max, down_all)
                if ffn:
                    low(2)
                    low(3)
                if first:
                    wkv_numerator(i + 1)
                if last:
                    mask_low(0)
                if att:
                    root("att", "varn", 3, i - 1)
                if last:
                    mask_low(1)
                if wkv:
                    root("wkv", "varn", 1, i + 1)
                if first:
                    all_max(slice(3, 6), moe_max, moe_all)
            pipeline(pool, run)

        @block.scalar
        def _(act):
            def norm(stage, names, k, src, dst, g):
                act.wait_ge(S[stage + "_dve"], after(stage + "_dve", names, g))
                pass_wait(act, act_passed, g)
                for b in range(GB):
                    nc.scalar.activation(dst[:, b, :], src(b), ACT.Identity,
                                         bias=shift[k][:, b:b + 1], scale=rstd[k][:, b:b + 1])\
                        .then_inc(S[stage + "_act"], 1)

            def wkv_exps(g):
                act.wait_ge(S["wkv_pe"], after("wkv_pe", "nT", g))
                if not (isinstance(g, int) and g == 0):
                    act.wait_ge(S["wkv_dve"], after("wkv_dve", "rden1", g - 1))
                for dst, bias in ((e1, neg_m), (e2, u_m)):
                    for k in range(KH):
                        nc.scalar.activation(dst[:, k * TW:(k + 1) * TW], tp_a[:, k * TW:(k + 1) * TW],
                                             ACT.Exp, bias=bias[:, k:k + 1])\
                            .then_inc(S["wkv_act"], 1)

            act.wait_ge(vec_in, 16)
            nc.scalar.activation(expd, vec[:, C_TD:C_TD + 2], ACT.Exp).then_inc(setup_act, 1)
            nc.scalar.activation(tg, vec[:, C_G:C_G + 4], ACT.Tanh).then_inc(setup_act, 1)
            act.wait_ge(setup_act, 1)
            nc.scalar.activation(lam, expd, ACT.Exp, scale=-1.0).then_inc(setup_act, 1)
            act.wait_ge(x0_in, 16)
            norm("wkv", "shift", 0, lambda b: xg(0, b), n1, 0)
            act.wait_ge(setup_dve, 1)
            wkv_exps(0)

            def prep_hi(n):
                w, half, c = chunk(n)
                if n in (0, 2):
                    act.wait_ge(ug_scaled, w + 1)
                act.wait_ge(prep_pe, arrived(n))
                nc.scalar.activation((up_h, gate_h)[w][0][:, half, c * 512:(c + 1) * 512],
                                     prep_bank[n][:, :], ACT.Copy, scale=sus[:, w, half:half + 1])\
                    .then_inc(prep_evac, 1)

            for n in by_arrival[:6]:
                prep_hi(n)
            norm("wkv", "shiftn", 1, lambda b: xg(0, b), n2, 0)
            for n in by_arrival[6:]:
                prep_hi(n)

            def run(i, ffn, wkv, att, last):
                first, second = (isinstance(i, int) and i == n for n in (0, 1))

                def copy(stage, src, dst):
                    nc.scalar.copy(dst, src).then_inc(S[stage + "_act"], 1)

                def ranks(j):
                    act.wait_ge(S["moe_pe"], after("moe_pe", f"h{j}", i - 1 - j))
                    nc.scalar.mul(hc[:, 2 * j:2 * j + 2, :],
                                  gate_p[j][:, :].rearrange("p (m t) -> p m t", m=2), M_SCALE)\
                        .then_inc(S["moe_act"], 1)

                def high(p):
                    act.wait_ge(S["ffn_dve"], after("ffn_dve", f"h{p}", i))
                    nc.scalar.copy(h_h[0][:, 2 * p:2 * p + 2, :],
                                   h_f[:, p % 2, :].rearrange("p (m t) -> p m t", m=2))\
                        .then_inc(S["ffn_act"], 1)

                def tanh(p):
                    act.wait_ge(S["ffn_pe"], after("ffn_pe", f"gate{p}", i))
                    if p >= 2:
                        act.wait_ge(S["ffn_dve"], after("ffn_dve", f"z{p - 2}", i))
                    for m in (2 * p, 2 * p + 1):
                        c = slice(m % 2 * TW, (m % 2 + 1) * TW)
                        nc.scalar.activation(tanh_g[:, p % 2, c], gate_p[p % 2][:, c], ACT.Tanh,
                                             scale=hwsg[:, m:m + 1]).then_inc(S["ffn_act"], 1)

                if ffn:
                    act.wait_ge(S["ffn_pe"], after("ffn_pe", "nT", i))
                    nc.scalar.mul(n2h[0][:, :, :], tp_a[:, :].rearrange("p (k t) -> p k t", k=KH), N_SCALE)\
                        .then_inc(S["ffn_act"], 1)
                if last:
                    ranks(1)
                    act.wait_ge(S["moe_pe"], after("moe_pe", "ohT", i - 2))
                    copy("moe", tp_b[0:EXPERTS, 0:GB * T // 2].bitcast(bf16), onehotT[:, :, :])
                if first:
                    act.wait_ge(setup_dve, 5)
                if ffn:
                    tanh(0)
                if wkv:
                    norm("wkv", "shift", 0, lambda b: xg(i + 1, b), n1, i + 1)
                if att:
                    norm("att", "shift", 2, lambda b: xg(i - 1, b), n3, i - 1)
                if ffn:
                    tanh(1)
                if wkv:
                    wkv_exps(i + 1)
                if second:
                    act.wait_ge(moe_scaled, 1)
                    for n, (w, h) in enumerate(((a_w, a_h), (b_w, b_h), (wg_w, wg_h))):
                        nc.scalar.activation(h[0][:, :, :], w[:, :, :], ACT.Copy,
                                             scale=wsc[:, n + 1:n + 2]).then_inc(moe_hi, 1)
                if ffn:
                    high(0)
                if att:
                    act.wait_ge(S["att_pe"], after("att_pe", "nT", i - 1))
                    copy("att", tp_b[:, :], n3T[:, :, :])
                if ffn:
                    high(1)
                    tanh(2)
                if att:
                    act.wait_ge(S["att_dve"], after("att_dve", "nbias", i - 1))
                    for b in range(GB):
                        nc.scalar.activation(prob[:, b, :], mix_p[:, b * T:(b + 1) * T], ACT.Exp,
                                             bias=nbias[:, b:b + 1], scale=D ** -0.5,
                                             accum_out=psum_row[:, b:b + 1])\
                            .then_inc(S["att_act"], 1)
                if ffn:
                    tanh(3)
                if att:
                    act.wait_ge(S["att_pe"], after("att_pe", "pT", i - 1))
                    copy("att", tp_b[:, 0:GB * T], probT[:, :, :])
                if ffn:
                    high(2)
                if first:
                    act.wait_ge(down_scaled, 1)
                    for m in (0, MI // 2):
                        nc.scalar.activation(down_h[0][:, m:m + MI // 2, :], w_down[:, m:m + MI // 2, :],
                                             ACT.Copy, scale=wsc[:, 0:1]).then_inc(down_hi, 1)
                if ffn:
                    high(3)
                if last:
                    for j in range(2):
                        act.wait_ge(S["moe_dve"], after("moe_dve", f"hm{j}", i - 2))
                        nc.scalar.copy(hm_h[0][:, 2 * j:2 * j + 2, :], hm_f[:, 2 * j:2 * j + 2, :])\
                            .then_inc(S["moe_act"], 1)
                if att:
                    norm("att", "shiftn", 3, lambda b: xg(i - 1, b), n4, i - 1)
                    act.wait_ge(S["moe_pe"], after("moe_pe", "nT", i - 1))
                    nc.scalar.mul(n4h[0][:, :, :], tp_b[:, :].rearrange("p (k t) -> p k t", k=KH), N_SCALE)\
                        .then_inc(S["moe_act"], 1)
                if wkv:
                    norm("wkv", "shiftn", 1, lambda b: xg(i + 1, b), n2, i + 1)
                if att:
                    act.wait_ge(S["moe_dve"], after("moe_dve", "diff", i - 1))
                    nc.scalar.activation(pexp[:, :, :], diff[:, :, :], ACT.Exp, scale=unsc[:, 2:3])\
                        .then_inc(S["moe_act"], 1)
                    ranks(0)
            pipeline(act, run)

        @block.vector
        def _(dve):
            def moments(stage, k, g, suffix=""):
                name, s = stage + "_dve", S[stage + "_dve"]
                pass_wait(dve, dve_passed, g)
                for b in range(GB):
                    nc.vector.bn_stats(st[k][:, b, :], xg(g, b)).then_inc(s, 1)
                dve.wait_ge(s, after(name, "stats1" + suffix, g))
                pass_wait(dve, dve_passed, g)
                for b in range(GB):
                    nc.vector.bn_aggr(mv[k][:, b, :], st[k][:, b, :]).then_inc(s, 1)
                dve.wait_ge(s, after(name, "aggr1" + suffix, g))
                nc.vector.tensor_scalar(var[k][:, :], mv[k][:, :, 1], LN_EPS, None, ALU.add).then_inc(s, 1)

            def offsets(stage, k, g, suffix=""):
                dve.wait_ge(S[stage + "_pool"], after(stage + "_pool", "rstd" + suffix, g))
                nc.vector.scalar_tensor_tensor(shift[k][:, :], mv[k][:, :, 0], -1.0, rstd[k][:, :],
                                               ALU.mult, ALU.mult).then_inc(S[stage + "_dve"], 1)

            def wkv_sums(g):
                s, name = S["wkv_dve"], "wkv_dve"
                vg = v_all[:, bass.ds(g * KH * TW, KH * TW)]
                dve.wait_ge(S["wkv_act"], after("wkv_act", "e1_1", g))
                nc.vector.tensor_tensor_scan(sum_b[:, 1:], decay[:, :], e1[:, :], 0.0,
                                             ALU.mult, ALU.add).then_inc(s, 1)
                pass_wait(dve, dve_passed, g)
                nc.vector.tensor_tensor(ev1[:, :], e1[:, :], vg, ALU.mult).then_inc(s, 1)
                dve.wait_ge(S["wkv_act"], after("wkv_act", "e2_1", g))
                dve.wait_ge(s, after(name, "scan_b", g))
                nc.vector.tensor_tensor(den[:, :], sum_b[:, 0:KH * TW], e2[:, :], ALU.add).then_inc(s, 1)
                dve.wait_ge(s, after(name, "ev1", g))
                nc.vector.tensor_tensor_scan(sum_a[:, 1:], decay[:, :], ev1[:, :], 0.0,
                                             ALU.mult, ALU.add).then_inc(s, 1)
                nc.vector.tensor_copy(y_t[:, :].rearrange("p (s t) -> p s t", t=T)[:, :, 0],
                                      vg.rearrange("p (s t) -> p s t", t=T)[:, :, 0]).then_inc(s, 1)

            def wkv_inverse(k, g):
                dve.wait_ge(S["wkv_dve"], after("wkv_dve", "den", g))
                nc.vector.reciprocal(rden[:, k * TW:(k + 1) * TW], den[:, k * TW:(k + 1) * TW])\
                    .then_inc(S["wkv_dve"], 1)

            def wkv_quotient(g):
                s, name = S["wkv_dve"], "wkv_dve"
                dve.wait_ge(S["wkv_pool"], after("wkv_pool", "num", g))
                dve.wait_ge(s, after(name, "rden1", g))
                y3, num3, rden3 = (t[:, :].rearrange("p (s t) -> p s t", t=T)[:, :, 1:]
                                   for t in (y_t, num, rden))
                nc.vector.tensor_tensor(y3, num3, rden3, ALU.mult).then_inc(s, 1)

            def wkv_residual(g):
                s = S["wkv_dve"]
                dve.wait_ge(S["wkv_pe"], after("wkv_pe", "yT", g))
                dve.wait_ge(S["wkv_act"], after("wkv_act", "norm1", g))
                nc.vector.scalar_tensor_tensor(xg(g), tp_a[:, :], tg[:, 0:1], xg(g), ALU.mult, ALU.add)\
                    .then_inc(s, 1)

            def largest(col, w, done):
                nc.vector.tensor_reduce(amax[:, col:col + 1], w, AX.XY, ALU.max,
                                        apply_absolute_value=True).then_inc(done, 1)

            def inverse(cols, done, k):
                nc.vector.tensor_scalar(gmax[:, cols], gmax[:, cols], TINY, None, ALU.max).then_inc(done, 1)
                dve.wait_ge(done, k + 1)
                nc.vector.reciprocal(ginv[:, cols], gmax[:, cols]).then_inc(done, 1)
                dve.wait_ge(done, k + 2)

            def row_scales(w, ready):
                dve.wait_ge(ready, 1)
                inverse(slice(w, w + 1), scale_steps, 2 * w)
                nc.vector.tensor_scalar(sus[:, w, :], vec[:, C_SUG:C_SUG + KH], ginv[:, w:w + 1],
                                        W_SCALE * D ** -0.5, ALU.mult, ALU.mult).then_inc(ug_scaled, 1)

            def prep_low(n):
                w, half, c = chunk(n)
                dst = (up_h, gate_h)[w]
                cc = slice(c * 512, (c + 1) * 512)
                dve.wait_ge(prep_evac, arrived(n))
                nc.vector.scalar_tensor_tensor(dst[1][:, half, cc], prep_bank[n][:, :],
                                               sus[:, w, half:half + 1], dst[0][:, half, cc],
                                               ALU.mult, ALU.subtract).then_inc(prep_lo, 1)

            dve.wait_ge(x0_in, 16)
            moments("wkv", 0, 0)
            offsets("wkv", 0, 0)
            dve.wait_ge(vec_in, 16)
            nc.vector.memset(decay[:, :], 1.0)
            nc.vector.memset(sum_b[:, 0:1], 1.0)
            nc.vector.memset(sum_a[:, 0:1], 0.0)
            nc.vector.tensor_scalar(neg_m, vec[:, C_U:C_U + 2], 0.0, -1.0, ALU.max, ALU.mult)
            nc.vector.tensor_scalar(u_m, vec[:, C_U:C_U + 2], 0.0, None, ALU.min).then_inc(setup_dve, 1)
            dve.wait_ge(setup_act, 3)
            dve.wait_ge(setup_dve, 1)
            for k in range(KH):
                nc.vector.tensor_scalar(decay[:, k * TW:(k + 1) * TW], decay[:, k * TW:(k + 1) * TW],
                                        lam[:, k:k + 1], None, ALU.mult).then_inc(setup_dve, 1)
            dve.wait_ge(setup_dve, 3)
            nc.vector.memset(decay[:, :].rearrange("p (s t) -> p s t", t=T)[:, :, 0], 0.0)\
                .then_inc(setup_dve, 1)
            dve.wait_ge(setup_dve, 4)
            dve.wait_ge(up_in, 16)
            largest(0, raw_up[:, :, :], up_max)
            dve.wait_ge(v0_in, 16)
            wkv_sums(0)
            row_scales(0, up_all)
            wkv_inverse(0, 0)
            wkv_inverse(1, 0)
            wkv_quotient(0)
            dve.wait_ge(gate_in, 16)
            largest(1, raw_gate[:, :, :], gate_max)
            wkv_residual(0)
            row_scales(1, gate_all)
            dve.wait_ge(S["wkv_dve"], after("wkv_dve", "x1", 0))
            moments("wkv", 1, 0, "n")
            prep_low(0)
            prep_low(1)
            offsets("wkv", 1, 0, "n")
            prep_low(2)
            prep_low(3)

            def setup_scales():
                nc.vector.tensor_scalar(hwsg, vec[:, C_WSG:C_WSG + MI], gmax[:, 1:2],
                                        0.5 / (N_SCALE * W_SCALE), ALU.mult, ALU.mult).then_inc(setup_dve, 1)
                nc.vector.tensor_scalar(frow, vec[:, C_SUD:C_SUD + MI], gmax[:, 0:1],
                                        1.0 / (N_SCALE * W_SCALE * H_SCALE), ALU.mult, ALU.mult)\
                    .then_inc(setup_dve, 1)
                nc.vector.tensor_scalar(wdp[:, :], vec[:, C_WDP:C_WDP + D], tg[:, 2:3], INTER ** -0.5,
                                        ALU.mult, ALU.mult).then_inc(setup_dve, 1)
                dve.wait_ge(setup_dve, 7)
                nc.vector.tensor_tensor(frow, frow, hwsg, ALU.mult).then_inc(setup_dve, 1)
                dve.wait_ge(setup_dve, 8)
                nc.vector.tensor_tensor(frow, frow, vec[:, C_WSU:C_WSU + MI], ALU.mult).then_inc(setup_dve, 1)
                dve.wait_ge(setup_dve, 9)

            def scale_down():
                for j in range(4):
                    dve.wait_ge(prep_down, j + 1)
                    for k in (2 * j, 2 * j + 1):
                        nc.vector.scalar_tensor_tensor(w_down[:, k, :],
                                                       down_bank[j][:, k % 2 * D:(k % 2 + 1) * D],
                                                       frow[:, k:k + 1], wdp[:, :], ALU.mult, ALU.mult)\
                            .then_inc(down_f32, 1)
                dve.wait_ge(down_f32, MI)
                largest(2, w_down[:, :, :], down_max)

            def down_factors():
                dve.wait_ge(down_all, 1)
                inverse(slice(2, 3), scale_steps, 4)
                nc.vector.tensor_scalar(wsc[:, 0:1], ginv[:, 2:3], L_SCALE, None, ALU.mult)
                nc.vector.tensor_scalar(unsc[:, 0:1], gmax[:, 2:3], 1 / L_SCALE, None, ALU.mult)\
                    .then_inc(down_scaled, 1)

            def down_low():
                for n, m in enumerate((0, MI // 2)):
                    dve.wait_ge(down_hi, n + 1)
                    nc.vector.scalar_tensor_tensor(down_h[1][:, m:m + MI // 2, :], w_down[:, m:m + MI // 2, :],
                                                   wsc[:, 0:1], down_h[0][:, m:m + MI // 2, :],
                                                   ALU.mult, ALU.subtract).then_inc(down_lo, 1)

            def measure_moe():
                dve.wait_ge(small_in, 16 * 6)
                for col, w in ((3, a_w), (4, b_w), (5, wg_w)):
                    nc.vector.tensor_reduce(amax[:, col:col + 1], w[:, :, :], AX.XY, ALU.max,
                                            apply_absolute_value=True).then_inc(moe_max, 1)

            def moe_factors():
                dve.wait_ge(moe_all, 1)
                inverse(slice(3, 6), scale_steps, 6)
                for n, c in ((1, A_SCALE), (2, L_SCALE), (3, L_SCALE)):
                    nc.vector.tensor_scalar(wsc[:, n:n + 1], ginv[:, n + 2:n + 3], c, None, ALU.mult)
                nc.vector.tensor_scalar(unsc[:, 2:3], gmax[:, 5:6], 1 / (N_SCALE * L_SCALE), None, ALU.mult)
                nc.vector.tensor_tensor(unsc[:, 1:2], gmax[:, 3:4], gmax[:, 4:5], ALU.mult)\
                    .then_inc(moe_scaled, 1)
                dve.wait_ge(moe_scaled, 1)
                nc.vector.tensor_scalar(tg4, tg[:, 3:4], unsc[:, 1:2],
                                        SCALING / (N_SCALE * A_SCALE * M_SCALE * L_SCALE),
                                        ALU.mult, ALU.mult).then_inc(setup_dve, 1)

            def moe_low_halves():
                for n, (w, h) in enumerate(((a_w, a_h), (b_w, b_h), (wg_w, wg_h))):
                    dve.wait_ge(moe_hi, n + 1)
                    nc.vector.scalar_tensor_tensor(h[1][:, :, :], w[:, :, :], wsc[:, n + 1:n + 2],
                                                   h[0][:, :, :], ALU.mult, ALU.subtract)\
                        .then_inc(moe_lo, 1)
                dve.wait_ge(setup_dve, 10)

            def run(i, ffn, wkv, att, last):
                def inner_z(p):
                    dve.wait_ge(S["ffn_act"], after("ffn_act", f"tanh{2 * p + 1}", i))
                    nc.vector.scalar_tensor_tensor(z_g[:, p % 2, :], tanh_g[:, p % 2, :], 1.0, gate_p[p % 2][:, :],
                                                   ALU.add, ALU.mult).then_inc(S["ffn_dve"], 1)

                def inner_h(p):
                    dve.wait_ge(S["ffn_dve"], after("ffn_dve", f"z{p}", i))
                    dve.wait_ge(S["ffn_pe"], after("ffn_pe", f"up{p}", i))
                    if p >= 2:
                        dve.wait_ge(S["ffn_pool"], after("ffn_pool", f"hlo{p - 2}", i))
                    nc.vector.scalar_tensor_tensor(h_f[:, p % 2, :], z_g[:, p % 2, :], H_SCALE, up_p[p % 2][:, :],
                                                   ALU.mult, ALU.mult).then_inc(S["ffn_dve"], 1)

                def inner(p):
                    inner_z(p)
                    inner_h(p)

                def low(dst, bank, stage):
                    dve.wait_ge(S[stage + "_act"], after(stage + "_act", "hi", i if stage == "ffn" else i - 1))
                    nc.vector.scalar_tensor_tensor(dst[1][:, :, :], bank[:, :].rearrange("p (k t) -> p k t", k=KH),
                                                   N_SCALE, dst[0][:, :, :], ALU.mult, ALU.subtract)\
                        .then_inc(S[stage + "_dve"], 1)

                first, second = (isinstance(i, int) and i == n for n in (0, 1))
                def masked(j):
                    g, bank = i - 2, (mix_p, tp_b)[j]
                    dve.wait_ge(S["moe_act"], after("moe_act", f"hc{j}", g))
                    dve.wait_ge(S["moe_pe"], after("moe_pe", f"mask{j}", g))
                    nc.vector.tensor_tensor(hm_f[:, 2 * j:2 * j + 2, :], hc[:, 2 * j:2 * j + 2, :],
                                            bank[:, :].rearrange("p (m t) -> p m t", m=2),
                                            ALU.mult).then_inc(S["moe_dve"], 1)

                if first:
                    setup_scales()
                if ffn:
                    low(n2h, tp_a, "ffn")
                if first:
                    for n in range(4, PREP):
                        prep_low(n)
                    dve.wait_ge(rest_in, 32)
                if wkv:
                    moments("wkv", 0, i + 1)
                if att:
                    dve.wait_ge(S["ffn_dve"], after("ffn_dve", "x2", i - 1))
                    moments("att", 2, i - 1)
                if wkv:
                    offsets("wkv", 0, i + 1)
                if last:
                    masked(0)
                if att:
                    offsets("att", 2, i - 1)
                if ffn:
                    inner_z(0)
                if ffn:
                    inner_h(0)
                if last:
                    masked(1)
                if second:
                    moe_factors()
                if ffn:
                    inner(1)
                if wkv:
                    wkv_sums(i + 1)
                if first:
                    scale_down()
                    inner(2)
                    down_factors()
                    inner(3)
                    down_low()
                if wkv:
                    wkv_inverse(0, i + 1)
                if att:
                    s, g = S["att_dve"], i - 1
                    dve.wait_ge(S["att_pe"], after("att_pe", "scores", g))
                    nc.vector.reduce_max(rmax, mix_p[:, 0:GB * T].rearrange("p (b t) -> p b t", b=GB),
                                         AX.X).then_inc(s, 1)
                    dve.wait_ge(s, after("att_dve", "rmax", g))
                    nc.vector.tensor_scalar(nbias, rmax, -(D ** -0.5), None, ALU.mult).then_inc(s, 1)
                    nc.vector.tensor_scalar(valid, rmax, MASKED / 2, tg[:, 1:2], ALU.is_gt, ALU.mult)\
                        .then_inc(s, 1)
                if ffn and not first:
                    inner(2)
                if att:
                    dve.wait_ge(S["att_act"], after("att_act", "exp1", g))
                    nc.vector.reciprocal(rsum, psum_row).then_inc(s, 1)
                    dve.wait_ge(s, after("att_dve", "rsum", g))
                    nc.vector.tensor_tensor(acoef, rsum, valid, ALU.mult).then_inc(s, 1)
                if second:
                    moe_low_halves()
                if ffn and not first:
                    inner(3)
                if att:
                    dve.wait_ge(S["att_pe"], after("att_pe", "pv", g))
                    dve.wait_ge(s, after("att_dve", "coef", g))
                    for b in range(GB):
                        nc.vector.scalar_tensor_tensor(xg(g, b), mix_p[:, b * D:(b + 1) * D],
                                                       acoef[:, b:b + 1], xg(g, b), ALU.mult, ALU.add)\
                            .then_inc(s, 1)
                    dve.wait_ge(s, after("att_dve", "x3_1", g))
                    moments("att", 3, g, "n")
                if wkv:
                    wkv_inverse(1, i + 1)
                if att:
                    offsets("att", 3, g, "n")
                if wkv:
                    wkv_quotient(i + 1)
                if ffn:
                    dve.wait_ge(S["ffn_pe"], after("ffn_pe", "down", i))
                    nc.vector.scalar_tensor_tensor(xg(i), down_p[:, :], unsc[:, 0:1], xg(i),
                                                   ALU.mult, ALU.add).then_inc(S["ffn_dve"], 1)
                if wkv:
                    wkv_residual(i + 1)
                    dve.wait_ge(S["wkv_dve"], after("wkv_dve", "x1", i + 1))
                    moments("wkv", 1, i + 1, "n")
                if att:
                    low(n4h, tp_b, "moe")
                if wkv:
                    offsets("wkv", 1, i + 1, "n")
                if first:
                    measure_moe()
                if last:
                    dve.wait_ge(S["out_pe"], after("out_pe", "y", i - 2))
                    for b in range(GB):
                        nc.vector.scalar_tensor_tensor(xg(i - 2, b), up_p[0][:, b * D:(b + 1) * D],
                                                       mcoef[:, b:b + 1], xg(i - 2, b), ALU.mult, ALU.add)\
                            .then_inc(S["out_dve"], 1)
                if att:
                    s, g = S["moe_dve"], i - 1
                    lg = mix_p[:, 0:GB * EXPERTS].rearrange("p (b e) -> p b e", b=GB)
                    rk = rank[:, :].rearrange("p (b e) -> p b e", b=GB)
                    dve.wait_ge(S["moe_pe"], after("moe_pe", "logits", g))
                    nc.vector.reduce_max(lmax, lg, AX.X).then_inc(s, 1)
                    dve.wait_ge(s, after("moe_dve", "lmax", g))
                    nc.vector.tensor_tensor(diff[:, :, :], lg, lmax.unsqueeze(2).broadcast_to([P, GB, EXPERTS]),
                                            ALU.subtract).then_inc(s, 1)
                    dve.wait_ge(s, after("moe_dve", "diff", g))
                    nc.vector.scalar_tensor_tensor(ranked[:, :, :], diff[:, :, :], 0.0, rk,
                                                   ALU.is_ge, ALU.mult).then_inc(s, 1)
                    dve.wait_ge(s, after("moe_dve", "ranked", g))
                    nc.vector.reduce_max(rtop, ranked[:, :, :], AX.X).then_inc(s, 1)
                    dve.wait_ge(s, after("moe_dve", "rtop", g))
                    nc.vector.tensor_tensor(onehot[:, :, :], ranked[:, :, :],
                                            rtop.unsqueeze(2).broadcast_to([P, GB, EXPERTS]),
                                            ALU.is_equal).then_inc(s, 1)
                if att:
                    dve.wait_ge(S["moe_act"], after("moe_act", "exp", g))
                    nc.vector.reduce_sum(msum, pexp[:, :, :], AX.X).then_inc(s, 1)
                    dve.wait_ge(s, after("moe_dve", "rsum", g))
                    nc.vector.reciprocal(mrinv, msum).then_inc(s, 1)
                    dve.wait_ge(s, after("moe_dve", "rinv", g))
                    nc.vector.tensor_scalar(mcoef, mrinv, tg4, None, ALU.mult).then_inc(s, 1)
            pipeline(dve, run)

        @block.tensor
        def _(pe):
            def to_channels(dst, src):
                for k in range(KH):
                    for b in range(GB):
                        c = k * TW + b * T
                        last = nc.tensor.transpose(dst[:, c:c + T], src[:, b, k * P:(k + 1) * P], ident[:, :])
                return last

            def y_to_tokens():
                for b in range(GB):
                    for k in range(KH):
                        last = nc.tensor.transpose(tp_a[:, b * D + k * P:b * D + (k + 1) * P],
                                                   y_t[:, k * TW + b * T:k * TW + (b + 1) * T], ident[:, :])
                return last

            def split_matmul(dst, lhs, rhs, first, last):
                for n, (a, b) in enumerate(((0, 0), (1, 0), (0, 1))):
                    o = nc.tensor.matmul(dst, lhs(a), rhs(b), start=first and n == 0, stop=last and n == 2)
                return o

            def prep(n):
                w, half, c = chunk(n)
                for k in range(KH):
                    sign = P if half and k else 0
                    last = nc.tensor.matmul(prep_bank[n][:, :], had[:, sign:sign + P],
                                            (raw_up, raw_gate)[w][:, k, c * 512:(c + 1) * 512],
                                            start=k == 0, stop=k == 1)
                last.then_inc(prep_pe, 1)

            pe.wait_ge(consts_in, 32)
            pe.wait_ge(S["wkv_act"], after("wkv_act", "norm1", 0))
            to_channels(tp_a, n1).then_inc(S["wkv_pe"], 1)
            pe.wait_ge(up_in, 16)
            for n in by_arrival[:4]:
                prep(n)
            pe.wait_ge(gate_in, 16)
            prep(by_arrival[4])
            pe.wait_ge(S["wkv_act"], after("wkv_act", "e2_1", 0))
            pe.wait_ge(S["wkv_dve"], after("wkv_dve", "y", 0))
            y_to_tokens().then_inc(S["wkv_pe"], 1)
            prep(by_arrival[5])
            prep(by_arrival[6])
            pe.wait_ge(prep_lo, 2)
            prep(by_arrival[7])

            def transform_down():
                pe.wait_ge(bfly_done, 6)
                for j in range(4):
                    if j == 3:
                        pe.wait_ge(down_f32, 2)
                    o = nc.tensor.matmul(down_bank[j][:, :], had[:, 0:P],
                                         bfly[:, 2 * j:2 * j + 2, :], start=True, stop=True)
                    o.then_inc(prep_down, 1)

            def run(i, ffn, wkv, att, last):
                def inner_product(w, p):
                    dst, weights, user = ((gate_p, gate_h, "z"), (up_p, up_h, "h"))[w]
                    if p >= 2:
                        pe.wait_ge(S["ffn_dve"], after("ffn_dve", f"{user}{p - 2}", i))
                    elif w == 0 and last:
                        pe.wait_ge(S["moe_act"], after("moe_act", f"hc{p}", i - 2))
                    for m in (2 * p, 2 * p + 1):
                        for k in range(KH):
                            o = split_matmul(dst[p % 2][:, m % 2 * TW:(m % 2 + 1) * TW],
                                             lambda a: weights[a][:, k, m * P:(m + 1) * P],
                                             lambda a: n2h[a][:, k, :], k == 0, k == KH - 1)
                    o.then_inc(S["ffn_pe"], 1)

                def ranks(j):
                    for m in (2 * j, 2 * j + 1):
                        for k in range(KH):
                            o = split_matmul(gate_p[j][:, m % 2 * TW:(m % 2 + 1) * TW],
                                             lambda a: a_h[a][:, k, m * P:(m + 1) * P],
                                             lambda a: n4h[a][:, k, :], k == 0, k == KH - 1)
                    o.then_inc(S["moe_pe"], 1)

                def mask(j, bank):
                    for m in (2 * j, 2 * j + 1):
                        o = nc.tensor.matmul(bank[:, m % 2 * TW:(m % 2 + 1) * TW],
                                             expand[:, m * P:(m + 1) * P], onehotT[:, :, :],
                                             start=True, stop=True)
                    o.then_inc(S["moe_pe"], 1)

                def down(b, steps):
                    for a, m in steps:
                        if first and b == a == 0 and m % (MI // 2) == 0:
                            pe.wait_ge(down_lo, m // (MI // 2) + 1)
                        if b == 0 and m % 2 == 0:
                            if a == 0:
                                pe.wait_ge(S["ffn_act"], after("ffn_act", f"hhi{m // 2}", i))
                            else:
                                pe.wait_ge(S["ffn_pool"], after("ffn_pool", f"hlo{m // 2}", i))
                        for w in range(2 - a):
                            o = nc.tensor.matmul(down_p[:, b * D:(b + 1) * D],
                                                 h_h[a][:, m, b * T:(b + 1) * T], down_h[w][:, m, :],
                                                 start=a == w == m == 0, stop=(a, m) == DOWN_STEPS[-1])
                    return o

                first, second = (isinstance(i, int) and i == n for n in (0, 1))
                g = i - 1
                if ffn:
                    pe.wait_ge(S["wkv_act"], after("wkv_act", "norm1n", i))
                    to_channels(tp_a, n2).then_inc(S["ffn_pe"], 1)
                if last:
                    e = i - 2
                    ranks(1)
                    pe.wait_ge(S["moe_dve"], after("moe_dve", "onehot", e))
                    for b in range(GB):
                        o = nc.tensor.transpose(tp_b[0:EXPERTS, b * T // 2:(b + 1) * T // 2].bitcast(bf16),
                                                onehot[:, b, :], ident_b[:, :])
                    o.then_inc(S["moe_pe"], 1)
                if ffn:
                    if first:
                        pe.wait_ge(prep_lo, 4)
                    pe.wait_ge(S["ffn_dve"], after("ffn_dve", "lo", i))
                    inner_product(0, 0)
                if last:
                    pe.wait_ge(S["moe_act"], after("moe_act", "ohT", e))
                    mask(0, mix_p)
                    mask(1, tp_b)
                if ffn:
                    inner_product(1, 0)
                    if first:
                        pe.wait_ge(prep_lo, PREP)
                    inner_product(0, 1)
                if wkv:
                    pe.wait_ge(S["wkv_act"], after("wkv_act", "norm1", i + 1))
                    to_channels(tp_a, n1).then_inc(S["wkv_pe"], 1)
                if ffn:
                    inner_product(1, 1)
                if first:
                    transform_down()
                if att:
                    if second:
                        pe.wait_ge(small_ready, 3)
                        pe.wait_ge(small_in, 16 * 6)
                    pe.wait_ge(S["att_act"], after("att_act", "norm1", g))
                    if last:
                        pe.wait_ge(S["moe_dve"], after("moe_dve", "hm1", e))
                    to_channels(tp_b, n3).then_inc(S["att_pe"], 1)
                if ffn:
                    inner_product(0, 2)
                    inner_product(1, 2)
                if att:
                    pe.wait_ge(S["att_act"], after("att_act", "nT", g))
                    for b in range(GB):
                        for k in range(KH):
                            nc.tensor.matmul(mix_p[:, b * T:(b + 1) * T], n3T[:, k, b * T:(b + 1) * T],
                                             v_all[:, bass.ds(g * GW + k * TW + b * T, T)],
                                             start=k == 0, stop=False)
                        o = nc.tensor.matmul(mix_p[:, b * T:(b + 1) * T], ones[:, :],
                                             mask_b[:, bass.ds(g * TW + b * T, T)],
                                             start=False, stop=True)
                    o.then_inc(S["att_pe"], 1)
                if ffn:
                    inner_product(0, 3)
                if ffn:
                    inner_product(1, 3)
                if att:
                    pe.wait_ge(S["att_act"], after("att_act", "exp1", g))
                    for b in range(GB):
                        o = nc.tensor.transpose(tp_b[:, b * T:(b + 1) * T], prob[:, b, :], ident[:, :])
                    o.then_inc(S["att_pe"], 1)
                if ffn:
                    down(0, DOWN_STEPS[:2])
                if att:
                    if second:
                        pe.wait_ge(ctx_in, 16)
                    pe.wait_ge(S["att_act"], after("att_act", "pT", g))
                    for b in range(GB):
                        o = nc.tensor.matmul(mix_p[:, b * D:(b + 1) * D], probT[:, b, :],
                                             c_all[:, bass.ds(g * GW + b * D, D)], start=True, stop=True)
                    o.then_inc(S["att_pe"], 1)
                if ffn:
                    down(0, DOWN_STEPS[2:])
                    down(1, DOWN_STEPS).then_inc(S["ffn_pe"], 1)
                if wkv:
                    pe.wait_ge(S["wkv_dve"], after("wkv_dve", "y", i + 1))
                    y_to_tokens().then_inc(S["wkv_pe"], 1)
                if att:
                    if second:
                        pe.wait_ge(moe_lo, 3)
                    pe.wait_ge(S["att_act"], after("att_act", "norm1n", g))
                    to_channels(tp_b, n4).then_inc(S["moe_pe"], 1)
                if last:
                    pe.wait_ge(S["moe_pool"], after("moe_pool", "mlo1", e))
                    for b in range(GB):
                        for m in range(ME):
                            o = split_matmul(up_p[0][:, b * D:(b + 1) * D],
                                             lambda a: hm_h[a][:, m, b * T:(b + 1) * T],
                                             lambda a: b_h[a][:, m, :], m == 0, m == ME - 1)
                    o.then_inc(S["out_pe"], 1)
                if att:
                    pe.wait_ge(S["moe_dve"], after("moe_dve", "lo", g))
                    for b in range(GB):
                        for k in range(KH):
                            o = split_matmul(mix_p[:, b * EXPERTS:(b + 1) * EXPERTS],
                                             lambda a: n4h[a][:, k, b * T:(b + 1) * T],
                                             lambda a: wg_h[a][:, k, :], k == 0, k == KH - 1)
                    o.then_inc(S["moe_pe"], 1)
                    ranks(0)
            pipeline(pe, run)


def kernel(x, ctx_2048, mask_BxS2_bk0, g_xattn, g_ffn, L0_xattn_time_decay, L0_xattn_time_first,
           L0_ffn_SU_ug, L0_ffn_SU_dp, L0_ffn_Wscale_ug, L0_ffn_Wscale_dp, L0_ffn_W_up,
           L0_ffn_W_gate, L0_ffn_W_down, L1_ffn_A, L1_ffn_Bw, L1_ffn_Wg):
    import numpy as np
    import concourse.bacc as bacc
    from concourse.bass_utils import run_bass_kernel_spmd

    c = np.ascontiguousarray

    def chunks(a):
        return c(a.reshape(a.shape[0] // P, P, a.shape[1]).transpose(1, 0, 2))

    def cols(v):
        return np.asarray(v).reshape(-1, P).T

    x, ctx = np.asarray(x), np.asarray(ctx_2048)
    gates = np.concatenate([np.asarray(g_xattn), np.asarray(g_ffn)])
    wug = np.asarray(L0_ffn_Wscale_ug)
    vecs = np.concatenate([
        cols(L0_xattn_time_decay), cols(L0_xattn_time_first), cols(L0_ffn_SU_ug), cols(L0_ffn_SU_dp),
        cols(wug[INTER:]), cols(wug[:INTER]), np.broadcast_to(gates, (P, 4)),
        np.broadcast_to(np.asarray(L0_ffn_Wscale_dp), (P, D))], axis=1)
    had = np.ones((1, 1), np.float32)
    while had.shape[0] < P:
        had = np.block([[had, had], [had, -had]])
    arrays = {
        "x_tok": c(x.transpose(1, 0, 2)).reshape(P, B * D),
        "ctx_tok": c(ctx.transpose(1, 0, 2)).reshape(P, B * D),
        "ctx_chan": c(ctx.reshape(GROUPS, GB, T, KH, P).transpose(4, 0, 3, 1, 2)).reshape(P, -1),
        "mask_row": np.asarray(mask_BxS2_bk0).reshape(1, B * T),
        "vecs": c(vecs),
        "w_up_t": chunks(np.asarray(L0_ffn_W_up).T),
        "w_gate_t": chunks(np.asarray(L0_ffn_W_gate).T),
        "w_down_t": chunks(np.asarray(L0_ffn_W_down).T),
        "a_t": chunks(np.asarray(L1_ffn_A).reshape(ER, D).T),
        "b_t": chunks(np.asarray(L1_ffn_Bw).transpose(0, 2, 1).reshape(ER, D)),
        "wg_t": chunks(np.asarray(L1_ffn_Wg).T),
        "hadamard": np.concatenate([had, -had], axis=1).astype(np.float32),
        "ident_in": np.eye(P, dtype=np.float32),
        "expand_in": np.repeat(np.eye(EXPERTS, dtype=np.float32), RANK, axis=1),
        "rank_in": np.broadcast_to(np.arange(EXPERTS, 0, -1, dtype=np.float32), (P, GB, EXPERTS)).reshape(P, -1).copy(),
    }
    nc = bacc.Bacc("TRN2", target_bir_lowering=False, num_devices=1)
    args = [nc.dram_tensor(n, a.shape, mybir.dt.from_np(a.dtype), kind="ExternalInput").ap()
            for n, a in arrays.items()]
    out = nc.dram_tensor("out_tok", (P, B * D), mybir.dt.float32, kind="ExternalOutput").ap()
    flamingo_kernel(nc, *args, out)
    r = run_bass_kernel_spmd(nc, [arrays], core_ids=[0])
    got = r.results[0]["out_tok"]
    return c(np.asarray(got).reshape(T, B, D).transpose(1, 0, 2))
```

```python
import concourse.bass as bass
from concourse import mybir
from contextlib import ExitStack

B, T, D = 16, 128, 256
INTER = 1024
EXPERTS, RANK = 8, 64
P = 128
KH = D // P
GB = 2
GROUPS = B // GB
GW = GB * D
TW = GB * T
MI = INTER // P
ER = EXPERTS * RANK
ME = ER // P
LN_EPS = 1e-5
MASKED = -1e30 * D ** 0.5
SCALING = 4.0
PREP = 4 * KH

N_SCALE = 2.0 ** 6
W_SCALE = 2.0 ** 6
H_SCALE = 2.0 ** -26
A_SCALE = 2.0 ** 8
M_SCALE = 2.0 ** -7
L_SCALE = 2.0 ** 14
DOWN_STEPS = [(a, m) for a in range(2) for m in range(MI)]
B_STEPS = [(a, m) for a in range(2) for m in range(ME)]
TINY = 1e-30

C_TD, C_U, C_SUG, C_SUD, C_WSG, C_WSU, C_G, C_WDP = 0, 2, 4, 6, 14, 22, 30, 34
VECS = C_WDP + D

STEPS = dict(
    wkv_dve="stats0 stats1 aggr0 aggr1 var shift scan_b ev1 scan_a y0 rden0 rden1 y x1 "
            "stats0n stats1n aggr0n aggr1n varn shiftn",
    wkv_pool="rstd den ev2 num rstdn",
    wkv_act="norm0 norm1 e1_0 e1_1 e2_0 e2_1 norm0n norm1n",
    wkv_pe="nT yT",
    ffn_pe="nT gate0 up0 gate1 up1 gate2 up2 gate3 up3 down",
    ffn_act="hi tanh0 tanh1 tanh2 tanh3 hhi0 hhi1 tanh4 tanh5 tanh6 tanh7 hhi2 hhi3",
    ffn_dve="lo z0 h0 z1 h1 z2 h2 z3 h3 x2",
    ffn_pool="hlo0 hlo1 hlo2 hlo3",
    att_pe="nT scores pT pv",
    att_act="norm0 norm1 nT exp0 exp1 pT norm0n norm1n",
    att_dve="stats0 stats1 aggr0 aggr1 var shift rmax nbias valid rsum coef x3_0 x3_1 "
            "stats0n stats1n aggr0n aggr1n varn shiftn",
    att_pool="rstd rstdn",
    moe_pe="nT logits h0 ohT h1 mask0 mask1",
    moe_act="hi exp hc0 ohT hc1 mhi0 mhi1",
    moe_dve="lo lmax diff ranked rtop onehot rsum rinv coef hm0 hm1",
    moe_pool="mlo0 mlo1",
    out_pe="y",
    out_dve="x4_0 x4_1",
)
STEPS = {k: v.split() for k, v in STEPS.items()}


def after(stage, step, g):
    return g * len(STEPS[stage]) + (STEPS[stage].index(step) + 1)


def flamingo_kernel(nc, x_tok, ctx_tok, ctx_chan, mask_row, vecs, w_up_t, w_gate_t, w_down_t,
                    a_t, b_t, wg_t, hadamard, ident_in, expand_in, rank_in, out_tok):
    fp32 = mybir.dt.float32
    bf16 = mybir.dt.bfloat16
    f16 = mybir.dt.float16
    u8 = mybir.dt.uint8
    ALU = mybir.AluOpType
    ACT = mybir.ActivationFunctionType
    AX = mybir.AxisListType

    ctx = ExitStack()
    with ctx:
        def sb(name, shape, dt=fp32):
            return ctx.enter_context(nc.sbuf_tensor(name, shape, dt))

        def pb(name):
            return ctx.enter_context(nc.psum_tensor(name, [P, 512], fp32))

        x_all = sb("x_all", [P, GROUPS * GW])
        c_all = sb("c_all", [P, GROUPS * GW])
        v_all = sb("v_all", [P, GROUPS * KH * TW])

        vec = sb("vec", [P, VECS])
        had = sb("had", [P, 2 * P])
        ident = sb("ident", [P, P])
        ident_b = sb("ident_b", [P, P], bf16)
        raw_up = sb("raw_up", [P, KH, INTER])
        raw_gate = sb("raw_gate", [P, KH, INTER])
        raw_down = sb("raw_down", [P, MI, D])
        bfly = sb("bfly", [P, MI, D])
        w_down = raw_up[:, :, :].rearrange("p k (m d) -> p (k m) d", d=D)
        a_w = sb("a_w", [P, KH, ER])
        b_w = sb("b_w", [P, ME, D])
        wg_w = sb("wg_w", [P, KH, EXPERTS])
        up_h = [sb(f"up_h{k}", [P, KH, INTER], f16) for k in range(2)]
        gate_h = [sb(f"gate_h{k}", [P, KH, INTER], f16) for k in range(2)]
        down_h = [sb(f"down_h{k}", [P, MI, D], f16) for k in range(2)]
        a_h = [sb(f"a_h{k}", [P, KH, ER], f16) for k in range(2)]
        b_h = [sb(f"b_h{k}", [P, ME, D], f16) for k in range(2)]
        wg_h = [sb(f"wg_h{k}", [P, KH, EXPERTS], f16) for k in range(2)]
        expand_f = sb("expand_f", [EXPERTS, ER])
        expand = sb("expand", [EXPERTS, ER], bf16)
        rank = sb("rank", [P, GB * EXPERTS])
        mask_u = sb("mask_u", [1, B * T], u8)
        mask_b = sb("mask_b", [1, B * T], bf16)
        ones = sb("ones", [1, P], bf16)
        decay = sb("decay", [P, KH * TW])
        small = sb("small", [P, 40])
        expd, lam = small[:, 0:2], small[:, 2:4]
        neg_m, u_m = small[:, 4:6], small[:, 6:8]
        tg = small[:, 8:12]
        tg4 = small[:, 12:13]
        hwsg = small[:, 16:24]
        frow = small[:, 24:32]
        amax = sb("amax", [P, 6])
        gmax = sb("gmax", [P, 6])
        ginv = sb("ginv", [P, 6])
        sus = sb("sus", [P, 2, KH])
        wsc = sb("wsc", [P, 4])
        unsc = sb("unsc", [P, 3])
        wdp = sb("wdp", [P, D])
        neg_half = sb("neg_half", [P, GB])

        n1, n2, n3, n4 = (sb(f"n{k}", [P, GB, D]) for k in (1, 2, 3, 4))
        n3T = sb("n3T", [P, KH, TW])
        n2h, n4h = ([sb(f"n{k}h{j}", [P, KH, TW], f16) for j in range(2)] for k in (2, 4))
        st = [sb(f"st{k}", [P, GB, 6]) for k in range(4)]
        mv = [sb(f"mv{k}", [P, GB, 2]) for k in range(4)]
        var = [sb(f"var{k}", [P, GB]) for k in range(4)]
        rstd = [sb(f"rstd{k}", [P, GB]) for k in range(4)]
        shift = [sb(f"shift{k}", [P, GB]) for k in range(4)]
        e1 = sb("e1", [P, KH * TW])
        e2 = sb("e2", [P, KH * TW])
        ev1 = sb("ev1", [P, KH * TW])
        ev2 = sb("ev2", [P, KH * TW])
        sum_b = sb("sum_b", [P, 1 + KH * TW])
        sum_a = sb("sum_a", [P, 1 + KH * TW])
        den = sb("den", [P, KH * TW])
        num = sb("num", [P, KH * TW])
        rden = sb("rden", [P, KH * TW])
        y_t = sb("y_t", [P, KH * TW])
        tanh_g = sb("tanh_g", [P, 2, 2 * TW])
        z_g = sb("z_g", [P, 2, 2 * TW])
        h_f = sb("h_f", [P, 2, 2 * TW])
        h_h = [sb(f"h_h{k}", [P, MI, TW], f16) for k in range(2)]
        prob = sb("prob", [P, GB, T])
        probT = sb("probT", [P, GB, T])
        att = sb("att", [P, 16])
        rmax, nbias, valid = att[:, 0:2], att[:, 2:4], att[:, 4:6]
        psum_row, rsum, acoef = att[:, 6:8], att[:, 8:10], att[:, 10:12]
        moe = sb("moe", [P, 16])
        lmax, rtop, msum, mrinv, mcoef = (moe[:, 2 * k:2 * k + 2] for k in range(5))
        diff = sb("diff", [P, GB, EXPERTS])
        pexp = sb("pexp", [P, GB, EXPERTS])
        ranked = sb("ranked", [P, GB, EXPERTS])
        onehot = sb("onehot", [P, GB, EXPERTS], bf16)
        onehotT = sb("onehotT", [EXPERTS, GB, T], bf16)
        hc, hm_f = (raw_gate[:, k, :].rearrange("p (m t) -> p m t", t=TW) for k in range(2))
        hm_h = [sb(f"hm_h{k}", [P, ME, TW], f16) for k in range(2)]

        tp_a = pb("tp_a")
        tp_b = pb("tp_b")
        gate_p = [pb("gate_p0"), pb("gate_p1")]
        up_p = [pb("up_p0"), pb("up_p1")]
        down_p = pb("down_p")
        mix_p = pb("mix_p")

        def sem(name):
            return ctx.enter_context(nc.semaphore(name))

        S = {k: sem(k) for k in STEPS}
        x0_in, vec_in, v0_in = sem("x0_in"), sem("vec_in"), sem("v0_in")
        consts_in = sem("consts_in")
        up_in, gate_in, down_in = sem("up_in"), sem("gate_in"), sem("down_in")
        rest_in = sem("rest_in")
        small_in = sem("small_in")
        ctx_in = sem("ctx_in")
        setup_act, setup_dve, setup_pool = sem("setup_act"), sem("setup_dve"), sem("setup_pool")
        prep_pe, prep_evac = sem("prep_pe"), sem("prep_evac")
        prep_lo = sem("prep_lo")
        up_max, gate_max, down_max, moe_max = (sem(f"{k}_max") for k in ("up", "gate", "down", "moe"))
        up_all, gate_all, down_all, moe_all = (sem(f"{k}_all") for k in ("up", "gate", "down", "moe"))
        ug_scaled, down_scaled, moe_scaled = (sem(f"{k}_scaled") for k in ("ug", "down", "moe"))
        prep_down, down_f32 = sem("prep_down"), sem("down_f32")
        down_hi, down_lo, moe_hi, moe_lo = (sem(k) for k in ("down_hi", "down_lo", "moe_hi", "moe_lo"))
        bfly_done, small_ready = sem("bfly_done"), sem("small_ready")
        stored = sem("stored")
        scale_steps = sem("scale_steps")
        act_passed, dve_passed, pool_passed = sem("act_passed"), sem("dve_passed"), sem("pool_passed")

        block = ctx.enter_context(nc.Block())

        def pass_wait(eng, passed, g):
            if not isinstance(g, int):
                eng.sem_inc(passed, 1)

        def xg(g, b=None):
            if b is None:
                return x_all[:, bass.ds(g * GW, GW)]
            return x_all[:, bass.ds(g * GW + b * D, D)]

        prep_bank = [gate_p[0], gate_p[1], up_p[0], up_p[1], down_p, mix_p, tp_b, gate_p[1]]
        down_bank = [tp_b, mix_p, down_p, tp_b]
        by_arrival = [0, 1, 4, 5, 2, 3, 6, 7]

        def chunk(n):
            return n // 2 % 2, n % 2, n // 4

        def arrived(n):
            return by_arrival.index(n) + 1

        moe_weights = [(a_w, a_h, 1), (wg_w, wg_h, 3), (b_w, b_h, 2)]

        def butterfly(eng, s, half):
            src, dst = ((raw_down, bfly), (bfly, raw_down))[s % 4 // 2]
            a = src[:, :, :].rearrange("p (x s y) d -> p x s (y d)", s=2, y=s)
            o = dst[:, :, :].rearrange("p (x s y) d -> p x s (y d)", s=2, y=s)
            eng.tensor_tensor(o[:, :, half], a[:, :, 0], a[:, :, 1],
                                    (ALU.add, ALU.subtract)[half]).then_inc(bfly_done, 1)

        def mask_banks(ffn):
            return (mix_p, tp_b) if ffn else (down_p, up_p[1])

        def choice_bank(ffn):
            return tp_b if ffn else tp_a

        def pipeline(eng, run):
            def flags(i):
                return dict(ffn=i < GROUPS, wkv=i + 1 < GROUPS, att=1 <= i <= GROUPS, last=i >= 2)
            for i in (0, 1):
                run(i, **flags(i))
            with eng.Fori(2, GROUPS - 1) as i:
                run(i, **flags(2))
            for i in range(GROUPS - 1, GROUPS + 2):
                run(i, **flags(i))

        @block.sync
        def _(sp):
            sp.dma_start(x_all[:, 0:GW], x_tok[:, 0:GW]).then_inc(x0_in, 16)
            sp.dma_start(vec[:, :], vecs).then_inc(vec_in, 16)
            sp.dma_start(ident[:, :], ident_in).then_inc(consts_in, 16)
            sp.dma_start(v_all[:, 0:GW], ctx_chan[:, 0:GW]).then_inc(v0_in, 16)
            sp.dma_start(had[:, :], hadamard).then_inc(consts_in, 16)
            sp.dma_start(raw_up[:, :, :], w_up_t).then_inc(up_in, 16)
            sp.dma_start(raw_gate[:, :, :], w_gate_t).then_inc(gate_in, 16)
            sp.dma_start(raw_down[:, :, :], w_down_t).then_inc(down_in, 16)
            sp.dma_start(x_all[:, GW:], x_tok[:, GW:]).then_inc(rest_in, 16)
            sp.dma_start(v_all[:, GW:], ctx_chan[:, GW:]).then_inc(rest_in, 16)
            sp.dma_start(mask_u[:, :], mask_row).then_inc(small_in, 16)
            sp.dma_start(expand_f[:, :], expand_in).then_inc(small_in, 16)
            sp.dma_start(rank[:, :], rank_in).then_inc(small_in, 16)
            sp.dma_start(a_w[:, :, :], a_t).then_inc(small_in, 16)
            sp.dma_start(b_w[:, :, :], b_t).then_inc(small_in, 16)
            sp.dma_start(wg_w[:, :, :], wg_t).then_inc(small_in, 16)
            sp.dma_start(c_all[:, :], ctx_tok).then_inc(ctx_in, 16)

            def run(i, ffn, wkv, att, last):
                if last:
                    g = i - 2
                    sp.wait_ge(S["out_dve"], after("out_dve", "x4_1", g))
                    sp.dma_start(out_tok[:, bass.ds(g * GW, GW)], xg(g)).then_inc(stored, 16)
            pipeline(sp, run)
            sp.wait_ge(stored, 16 * GROUPS)

        @block.gpsimd
        def _(pool):
            pool.memset(neg_half[:, :], -0.5)
            pool.memset(ones[:, :], 1.0).then_inc(setup_pool, 1)

            def root(stage, src, k, g):
                pool.wait_ge(S[stage + "_dve"], after(stage + "_dve", src, g))
                nc.gpsimd.tensor_tensor(rstd[k][:, :], var[k][:, :], neg_half[:, :], ALU.pow)\
                    .then_inc(S[stage + "_pool"], 1)

            def wkv_denominator(g):
                pool.wait_ge(S["wkv_act"], after("wkv_act", "e2_1", g))
                pool.wait_ge(S["wkv_dve"], after("wkv_dve", "scan_b", g))
                nc.gpsimd.tensor_tensor(den[:, :], sum_b[:, 0:KH * TW], e2[:, :], ALU.add)\
                    .then_inc(S["wkv_pool"], 1)

            def wkv_weighted(g):
                pass_wait(pool, pool_passed, g)
                nc.gpsimd.tensor_tensor(ev2[:, :], e2[:, :], v_all[:, bass.ds(g * KH * TW, KH * TW)],
                                        ALU.mult).then_inc(S["wkv_pool"], 1)

            def wkv_numerator(g):
                pool.wait_ge(S["wkv_dve"], after("wkv_dve", "scan_a", g))
                pool.wait_ge(S["wkv_pool"], after("wkv_pool", "ev2", g))
                nc.gpsimd.tensor_tensor(num[:, :], sum_a[:, 0:KH * TW], ev2[:, :], ALU.add)\
                    .then_inc(S["wkv_pool"], 1)

            def all_max(cols, ready, done):
                pool.wait_ge(ready, cols.stop - cols.start)
                nc.gpsimd.partition_all_reduce(gmax[:, cols], amax[:, cols], P, bass.bass_isa.ReduceOp.max)\
                    .then_inc(done, 1)

            pool.wait_ge(setup_pool, 1)
            root("wkv", "var", 0, 0)
            all_max(slice(0, 1), up_max, up_all)
            pool.wait_ge(v0_in, 16)
            wkv_denominator(0)
            wkv_weighted(0)
            wkv_numerator(0)
            pool.wait_ge(down_in, 16)
            butterfly(nc.gpsimd, 1, 0)
            all_max(slice(1, 2), gate_max, gate_all)
            butterfly(nc.gpsimd, 1, 1)
            root("wkv", "varn", 1, 0)
            pool.wait_ge(bfly_done, 2)
            butterfly(nc.gpsimd, 2, 0)
            pool.wait_ge(bfly_done, 4)
            butterfly(nc.gpsimd, 4, 0)
            butterfly(nc.gpsimd, 4, 1)

            def setup_small():
                pool.wait_ge(small_in, 16 * 6)
                nc.gpsimd.tensor_scalar(mask_b[:, :], mask_u[:, :], -1.0, -MASKED, ALU.add, ALU.mult)\
                    .then_inc(small_ready, 1)
                nc.gpsimd.tensor_copy(ident_b[:, :], ident[:, :]).then_inc(small_ready, 1)
                nc.gpsimd.tensor_copy(expand[:, :], expand_f[:, :]).then_inc(small_ready, 1)

            def run(i, ffn, wkv, att, last):
                def low(p):
                    pool.wait_ge(S["ffn_act"], after("ffn_act", f"hhi{p}", i))
                    nc.gpsimd.tensor_tensor(h_h[1][:, 2 * p:2 * p + 2, :],
                                            h_f[:, p % 2, :].rearrange("p (m t) -> p m t", m=2),
                                            h_h[0][:, 2 * p:2 * p + 2, :], ALU.subtract)\
                        .then_inc(S["ffn_pool"], 1)

                first, second = (isinstance(i, int) and i == n for n in (0, 1))
                if wkv:
                    root("wkv", "var", 0, i + 1)
                if att and ffn:
                    root("att", "var", 2, i - 1)
                def mask_low(j):
                    pool.wait_ge(S["moe_act"], after("moe_act", f"mhi{j}", i - 2))
                    nc.gpsimd.tensor_tensor(hm_h[1][:, 2 * j:2 * j + 2, :], hm_f[:, 2 * j:2 * j + 2, :],
                                            hm_h[0][:, 2 * j:2 * j + 2, :], ALU.subtract)\
                        .then_inc(S["moe_pool"], 1)

                if first:
                    setup_small()
                    low(0)
                    low(1)
                    all_max(slice(2, 3), down_max, down_all)
                    pool.wait_ge(rest_in, 32)
                if wkv:
                    wkv_denominator(i + 1)
                if ffn and not first:
                    low(0)
                if wkv:
                    wkv_weighted(i + 1)
                if ffn and not first:
                    low(1)
                if wkv:
                    wkv_numerator(i + 1)
                if ffn:
                    low(2)
                    low(3)
                if last:
                    mask_low(0)
                if last and not ffn:
                    mask_low(1)
                if att:
                    root("att", "varn", 3, i - 1)
                if last and ffn:
                    mask_low(1)
                if wkv:
                    root("wkv", "varn", 1, i + 1)
                if first:
                    all_max(slice(3, 6), moe_max, moe_all)
                if ffn and not wkv:
                    root("att", "var", 2, i)
            pipeline(pool, run)

        @block.scalar
        def _(act):
            def norm(stage, names, k, src, dst, g):
                act.wait_ge(S[stage + "_dve"], after(stage + "_dve", names, g))
                pass_wait(act, act_passed, g)
                for b in range(GB):
                    nc.scalar.activation(dst[:, b, :], src(b), ACT.Identity,
                                         bias=shift[k][:, b:b + 1], scale=rstd[k][:, b:b + 1])\
                        .then_inc(S[stage + "_act"], 1)

            def wkv_exps(g):
                act.wait_ge(S["wkv_pe"], after("wkv_pe", "nT", g))
                if not (isinstance(g, int) and g == 0):
                    act.wait_ge(S["wkv_dve"], after("wkv_dve", "rden1", g - 1))
                for dst, bias in ((e1, neg_m), (e2, u_m)):
                    for k in range(KH):
                        nc.scalar.activation(dst[:, k * TW:(k + 1) * TW], tp_a[:, k * TW:(k + 1) * TW],
                                             ACT.Exp, bias=bias[:, k:k + 1])\
                            .then_inc(S["wkv_act"], 1)

            act.wait_ge(vec_in, 16)
            nc.scalar.activation(expd, vec[:, C_TD:C_TD + 2], ACT.Exp).then_inc(setup_act, 1)
            nc.scalar.activation(tg, vec[:, C_G:C_G + 4], ACT.Tanh).then_inc(setup_act, 1)
            act.wait_ge(setup_act, 1)
            nc.scalar.activation(lam, expd, ACT.Exp, scale=-1.0).then_inc(setup_act, 1)
            act.wait_ge(x0_in, 16)
            norm("wkv", "shift", 0, lambda b: xg(0, b), n1, 0)
            act.wait_ge(setup_dve, 1)
            wkv_exps(0)

            def prep_hi(n):
                w, half, c = chunk(n)
                if n in (0, 2):
                    act.wait_ge(ug_scaled, w + 1)
                act.wait_ge(prep_pe, arrived(n))
                nc.scalar.activation((up_h, gate_h)[w][0][:, half, c * 512:(c + 1) * 512],
                                     prep_bank[n][:, :], ACT.Copy, scale=sus[:, w, half:half + 1])\
                    .then_inc(prep_evac, 1)

            for n in by_arrival[:6]:
                prep_hi(n)
            norm("wkv", "shiftn", 1, lambda b: xg(0, b), n2, 0)
            for n in by_arrival[6:]:
                prep_hi(n)

            def run(i, ffn, wkv, att, last):
                first, second = (isinstance(i, int) and i == n for n in (0, 1))

                def copy(stage, src, dst):
                    nc.scalar.copy(dst, src).then_inc(S[stage + "_act"], 1)

                def queries():
                    act.wait_ge(S["att_pe"], after("att_pe", "nT", i - 1))
                    copy("att", tp_b[:, :], n3T[:, :, :])

                def ranks(j):
                    act.wait_ge(S["moe_pe"], after("moe_pe", f"h{j}", i - 1 - j))
                    nc.scalar.mul(hc[:, 2 * j:2 * j + 2, :],
                                  gate_p[j][:, :].rearrange("p (m t) -> p m t", m=2), M_SCALE)\
                        .then_inc(S["moe_act"], 1)

                def high(p):
                    act.wait_ge(S["ffn_dve"], after("ffn_dve", f"h{p}", i))
                    nc.scalar.copy(h_h[0][:, 2 * p:2 * p + 2, :],
                                   h_f[:, p % 2, :].rearrange("p (m t) -> p m t", m=2))\
                        .then_inc(S["ffn_act"], 1)

                def tanh(p):
                    act.wait_ge(S["ffn_pe"], after("ffn_pe", f"gate{p}", i))
                    if p >= 2:
                        act.wait_ge(S["ffn_dve"], after("ffn_dve", f"z{p - 2}", i))
                    for m in (2 * p, 2 * p + 1):
                        c = slice(m % 2 * TW, (m % 2 + 1) * TW)
                        nc.scalar.activation(tanh_g[:, p % 2, c], gate_p[p % 2][:, c], ACT.Tanh,
                                             scale=hwsg[:, m:m + 1]).then_inc(S["ffn_act"], 1)

                if ffn:
                    act.wait_ge(S["ffn_pe"], after("ffn_pe", "nT", i))
                    nc.scalar.mul(n2h[0][:, :, :], tp_a[:, :].rearrange("p (k t) -> p k t", k=KH), N_SCALE)\
                        .then_inc(S["ffn_act"], 1)
                if att and not ffn:
                    queries()
                if last:
                    act.wait_ge(S["moe_pe"], after("moe_pe", "ohT", i - 2))
                    copy("moe", choice_bank(ffn)[0:EXPERTS, 0:GB * T // 2].bitcast(bf16), onehotT[:, :, :])
                    ranks(1)
                if first:
                    act.wait_ge(setup_dve, 5)
                if ffn:
                    tanh(0)
                if wkv:
                    norm("wkv", "shift", 0, lambda b: xg(i + 1, b), n1, i + 1)
                if att and ffn:
                    norm("att", "shift", 2, lambda b: xg(i - 1, b), n3, i - 1)
                if ffn:
                    tanh(1)
                if wkv:
                    wkv_exps(i + 1)
                if second:
                    act.wait_ge(moe_scaled, 1)
                    for w, h, c in moe_weights:
                        nc.scalar.activation(h[0][:, :, :], w[:, :, :], ACT.Copy,
                                             scale=wsc[:, c:c + 1]).then_inc(moe_hi, 1)
                if ffn:
                    high(0)
                if att and ffn:
                    queries()
                if ffn:
                    high(1)
                    tanh(2)
                if att:
                    act.wait_ge(S["att_dve"], after("att_dve", "nbias", i - 1))
                    for b in range(GB):
                        nc.scalar.activation(prob[:, b, :], mix_p[:, b * T:(b + 1) * T], ACT.Exp,
                                             bias=nbias[:, b:b + 1], scale=D ** -0.5,
                                             accum_out=psum_row[:, b:b + 1])\
                            .then_inc(S["att_act"], 1)
                if ffn:
                    tanh(3)
                if att:
                    act.wait_ge(S["att_pe"], after("att_pe", "pT", i - 1))
                    copy("att", tp_b[:, 0:GB * T], probT[:, :, :])
                if ffn and not first:
                    high(2)
                if first:
                    act.wait_ge(down_scaled, 1)
                    for m in (0, MI // 2):
                        nc.scalar.activation(down_h[0][:, m:m + MI // 2, :], w_down[:, m:m + MI // 2, :],
                                             ACT.Copy, scale=wsc[:, 0:1]).then_inc(down_hi, 1)
                    high(2)
                if ffn:
                    high(3)
                if last:
                    for j in range(2):
                        act.wait_ge(S["moe_dve"], after("moe_dve", f"hm{j}", i - 2))
                        nc.scalar.copy(hm_h[0][:, 2 * j:2 * j + 2, :], hm_f[:, 2 * j:2 * j + 2, :])\
                            .then_inc(S["moe_act"], 1)
                if att:
                    norm("att", "shiftn", 3, lambda b: xg(i - 1, b), n4, i - 1)
                    act.wait_ge(S["moe_pe"], after("moe_pe", "nT", i - 1))
                    nc.scalar.mul(n4h[0][:, :, :], tp_b[:, :].rearrange("p (k t) -> p k t", k=KH), N_SCALE)\
                        .then_inc(S["moe_act"], 1)
                if ffn and not wkv:
                    norm("att", "shift", 2, lambda b: xg(i, b), n3, i)
                if wkv:
                    norm("wkv", "shiftn", 1, lambda b: xg(i + 1, b), n2, i + 1)
                if att:
                    act.wait_ge(S["moe_dve"], after("moe_dve", "diff", i - 1))
                    nc.scalar.activation(pexp[:, :, :], diff[:, :, :], ACT.Exp, scale=unsc[:, 2:3])\
                        .then_inc(S["moe_act"], 1)
                    ranks(0)
            pipeline(act, run)

        @block.vector
        def _(dve):
            def moments(stage, k, g, suffix=""):
                name, s = stage + "_dve", S[stage + "_dve"]
                pass_wait(dve, dve_passed, g)
                for b in range(GB):
                    nc.vector.bn_stats(st[k][:, b, :], xg(g, b)).then_inc(s, 1)
                dve.wait_ge(s, after(name, "stats1" + suffix, g))
                pass_wait(dve, dve_passed, g)
                for b in range(GB):
                    nc.vector.bn_aggr(mv[k][:, b, :], st[k][:, b, :]).then_inc(s, 1)
                dve.wait_ge(s, after(name, "aggr1" + suffix, g))
                nc.vector.tensor_scalar(var[k][:, :], mv[k][:, :, 1], LN_EPS, None, ALU.add).then_inc(s, 1)

            def offsets(stage, k, g, suffix=""):
                dve.wait_ge(S[stage + "_pool"], after(stage + "_pool", "rstd" + suffix, g))
                nc.vector.scalar_tensor_tensor(shift[k][:, :], mv[k][:, :, 0], -1.0, rstd[k][:, :],
                                               ALU.mult, ALU.mult).then_inc(S[stage + "_dve"], 1)

            def wkv_sums(g):
                s, name = S["wkv_dve"], "wkv_dve"
                vg = v_all[:, bass.ds(g * KH * TW, KH * TW)]
                dve.wait_ge(S["wkv_act"], after("wkv_act", "e1_1", g))
                nc.vector.tensor_tensor_scan(sum_b[:, 1:], decay[:, :], e1[:, :], 0.0,
                                             ALU.mult, ALU.add).then_inc(s, 1)
                pass_wait(dve, dve_passed, g)
                nc.vector.tensor_tensor(ev1[:, :], e1[:, :], vg, ALU.mult).then_inc(s, 1)
                dve.wait_ge(s, after(name, "ev1", g))
                nc.vector.tensor_tensor_scan(sum_a[:, 1:], decay[:, :], ev1[:, :], 0.0,
                                             ALU.mult, ALU.add).then_inc(s, 1)
                nc.vector.tensor_copy(y_t[:, :].rearrange("p (s t) -> p s t", t=T)[:, :, 0],
                                      vg.rearrange("p (s t) -> p s t", t=T)[:, :, 0]).then_inc(s, 1)

            def wkv_inverse(k, g):
                dve.wait_ge(S["wkv_pool"], after("wkv_pool", "den", g))
                nc.vector.reciprocal(rden[:, k * TW:(k + 1) * TW], den[:, k * TW:(k + 1) * TW])\
                    .then_inc(S["wkv_dve"], 1)

            def wkv_quotient(g):
                s, name = S["wkv_dve"], "wkv_dve"
                dve.wait_ge(S["wkv_pool"], after("wkv_pool", "num", g))
                dve.wait_ge(s, after(name, "rden1", g))
                y3, num3, rden3 = (t[:, :].rearrange("p (s t) -> p s t", t=T)[:, :, 1:]
                                   for t in (y_t, num, rden))
                nc.vector.tensor_tensor(y3, num3, rden3, ALU.mult).then_inc(s, 1)

            def wkv_residual(g):
                s = S["wkv_dve"]
                dve.wait_ge(S["wkv_pe"], after("wkv_pe", "yT", g))
                dve.wait_ge(S["wkv_act"], after("wkv_act", "norm1", g))
                nc.vector.scalar_tensor_tensor(xg(g), tp_a[:, :], tg[:, 0:1], xg(g), ALU.mult, ALU.add)\
                    .then_inc(s, 1)

            def largest(col, w, done):
                nc.vector.tensor_reduce(amax[:, col:col + 1], w, AX.XY, ALU.max,
                                        apply_absolute_value=True).then_inc(done, 1)

            def inverse(cols, done, k):
                nc.vector.tensor_scalar(gmax[:, cols], gmax[:, cols], TINY, None, ALU.max).then_inc(done, 1)
                dve.wait_ge(done, k + 1)
                nc.vector.reciprocal(ginv[:, cols], gmax[:, cols]).then_inc(done, 1)
                dve.wait_ge(done, k + 2)

            def row_scales(w, ready):
                dve.wait_ge(ready, 1)
                inverse(slice(w, w + 1), scale_steps, 2 * w)
                nc.vector.tensor_scalar(sus[:, w, :], vec[:, C_SUG:C_SUG + KH], ginv[:, w:w + 1],
                                        W_SCALE * D ** -0.5, ALU.mult, ALU.mult).then_inc(ug_scaled, 1)

            def prep_low(n):
                w, half, c = chunk(n)
                dst = (up_h, gate_h)[w]
                cc = slice(c * 512, (c + 1) * 512)
                dve.wait_ge(prep_evac, arrived(n))
                nc.vector.scalar_tensor_tensor(dst[1][:, half, cc], prep_bank[n][:, :],
                                               sus[:, w, half:half + 1], dst[0][:, half, cc],
                                               ALU.mult, ALU.subtract).then_inc(prep_lo, 1)

            dve.wait_ge(x0_in, 16)
            moments("wkv", 0, 0)
            offsets("wkv", 0, 0)
            dve.wait_ge(vec_in, 16)
            nc.vector.memset(decay[:, :], 1.0)
            nc.vector.memset(sum_b[:, 0:1], 1.0)
            nc.vector.memset(sum_a[:, 0:1], 0.0)
            nc.vector.tensor_scalar(neg_m, vec[:, C_U:C_U + 2], 0.0, -1.0, ALU.max, ALU.mult)
            nc.vector.tensor_scalar(u_m, vec[:, C_U:C_U + 2], 0.0, None, ALU.min).then_inc(setup_dve, 1)
            dve.wait_ge(setup_act, 3)
            dve.wait_ge(setup_dve, 1)
            for k in range(KH):
                nc.vector.tensor_scalar(decay[:, k * TW:(k + 1) * TW], decay[:, k * TW:(k + 1) * TW],
                                        lam[:, k:k + 1], None, ALU.mult).then_inc(setup_dve, 1)
            dve.wait_ge(setup_dve, 3)
            nc.vector.memset(decay[:, :].rearrange("p (s t) -> p s t", t=T)[:, :, 0], 0.0)\
                .then_inc(setup_dve, 1)
            dve.wait_ge(setup_dve, 4)
            dve.wait_ge(up_in, 16)
            largest(0, raw_up[:, :, :], up_max)
            dve.wait_ge(v0_in, 16)
            wkv_sums(0)
            row_scales(0, up_all)
            wkv_inverse(0, 0)
            wkv_inverse(1, 0)
            wkv_quotient(0)
            dve.wait_ge(gate_in, 16)
            largest(1, raw_gate[:, :, :], gate_max)
            wkv_residual(0)
            row_scales(1, gate_all)
            dve.wait_ge(S["wkv_dve"], after("wkv_dve", "x1", 0))
            moments("wkv", 1, 0, "n")
            prep_low(0)
            prep_low(1)
            offsets("wkv", 1, 0, "n")
            dve.wait_ge(bfly_done, 2)
            butterfly(nc.vector, 2, 1)
            prep_low(2)
            prep_low(3)

            def setup_scales():
                nc.vector.tensor_scalar(hwsg, vec[:, C_WSG:C_WSG + MI], gmax[:, 1:2],
                                        0.5 / (N_SCALE * W_SCALE), ALU.mult, ALU.mult).then_inc(setup_dve, 1)
                nc.vector.tensor_scalar(frow, vec[:, C_SUD:C_SUD + MI], gmax[:, 0:1],
                                        1.0 / (N_SCALE * W_SCALE * H_SCALE), ALU.mult, ALU.mult)\
                    .then_inc(setup_dve, 1)
                nc.vector.tensor_scalar(wdp[:, :], vec[:, C_WDP:C_WDP + D], tg[:, 2:3], INTER ** -0.5,
                                        ALU.mult, ALU.mult).then_inc(setup_dve, 1)
                dve.wait_ge(setup_dve, 7)
                nc.vector.tensor_tensor(frow, frow, hwsg, ALU.mult).then_inc(setup_dve, 1)
                dve.wait_ge(setup_dve, 8)
                nc.vector.tensor_tensor(frow, frow, vec[:, C_WSU:C_WSU + MI], ALU.mult).then_inc(setup_dve, 1)
                dve.wait_ge(setup_dve, 9)

            def scale_down(blocks):
                for j in blocks:
                    dve.wait_ge(prep_down, j + 1)
                    for k in (2 * j, 2 * j + 1):
                        nc.vector.scalar_tensor_tensor(w_down[:, k, :],
                                                       down_bank[j][:, k % 2 * D:(k % 2 + 1) * D],
                                                       frow[:, k:k + 1], wdp[:, :], ALU.mult, ALU.mult)\
                            .then_inc(down_f32, 1)

            def measure_down():
                dve.wait_ge(down_f32, MI)
                largest(2, w_down[:, :, :], down_max)

            def down_factors():
                dve.wait_ge(down_all, 1)
                inverse(slice(2, 3), scale_steps, 4)
                nc.vector.tensor_scalar(wsc[:, 0:1], ginv[:, 2:3], L_SCALE, None, ALU.mult)
                nc.vector.tensor_scalar(unsc[:, 0:1], gmax[:, 2:3], 1 / L_SCALE, None, ALU.mult)\
                    .then_inc(down_scaled, 1)

            def down_low(n):
                m = n * MI // 2
                dve.wait_ge(down_hi, n + 1)
                nc.vector.scalar_tensor_tensor(down_h[1][:, m:m + MI // 2, :], w_down[:, m:m + MI // 2, :],
                                               wsc[:, 0:1], down_h[0][:, m:m + MI // 2, :],
                                               ALU.mult, ALU.subtract).then_inc(down_lo, 1)

            def measure_moe():
                dve.wait_ge(small_in, 16 * 6)
                for col, w in ((3, a_w), (4, b_w), (5, wg_w)):
                    nc.vector.tensor_reduce(amax[:, col:col + 1], w[:, :, :], AX.XY, ALU.max,
                                            apply_absolute_value=True).then_inc(moe_max, 1)

            def moe_factors():
                dve.wait_ge(moe_all, 1)
                inverse(slice(3, 6), scale_steps, 6)
                for n, c in ((1, A_SCALE), (2, L_SCALE), (3, L_SCALE)):
                    nc.vector.tensor_scalar(wsc[:, n:n + 1], ginv[:, n + 2:n + 3], c, None, ALU.mult)
                nc.vector.tensor_scalar(unsc[:, 2:3], gmax[:, 5:6], 1 / (N_SCALE * L_SCALE), None, ALU.mult)
                nc.vector.tensor_tensor(unsc[:, 1:2], gmax[:, 3:4], gmax[:, 4:5], ALU.mult)\
                    .then_inc(moe_scaled, 1)
                dve.wait_ge(moe_scaled, 1)
                nc.vector.tensor_scalar(tg4, tg[:, 3:4], unsc[:, 1:2],
                                        SCALING / (N_SCALE * A_SCALE * M_SCALE * L_SCALE),
                                        ALU.mult, ALU.mult).then_inc(setup_dve, 1)

            def moe_low_halves(which):
                for n in which:
                    w, h, c = moe_weights[n]
                    dve.wait_ge(moe_hi, n + 1)
                    nc.vector.scalar_tensor_tensor(h[1][:, :, :], w[:, :, :], wsc[:, c:c + 1],
                                                   h[0][:, :, :], ALU.mult, ALU.subtract)\
                        .then_inc(moe_lo, 1)
                dve.wait_ge(setup_dve, 10)

            def run(i, ffn, wkv, att, last):
                def inner(p):
                    name, done = "ffn_dve", S["ffn_dve"]
                    dve.wait_ge(S["ffn_act"], after("ffn_act", f"tanh{2 * p + 1}", i))
                    nc.vector.scalar_tensor_tensor(z_g[:, p % 2, :], tanh_g[:, p % 2, :], 1.0,
                                                   gate_p[p % 2][:, :],
                                                   ALU.add, ALU.mult).then_inc(done, 1)
                    dve.wait_ge(done, after(name, f"z{p}", i))
                    dve.wait_ge(S["ffn_pe"], after("ffn_pe", f"up{p}", i))
                    if p >= 2:
                        dve.wait_ge(S["ffn_pool"], after("ffn_pool", f"hlo{p - 2}", i))
                    nc.vector.scalar_tensor_tensor(h_f[:, p % 2, :], z_g[:, p % 2, :], H_SCALE,
                                                   up_p[p % 2][:, :],
                                                   ALU.mult, ALU.mult).then_inc(done, 1)

                def low(dst, bank, stage):
                    dve.wait_ge(S[stage + "_act"], after(stage + "_act", "hi", i if stage == "ffn" else i - 1))
                    nc.vector.scalar_tensor_tensor(dst[1][:, :, :],
                                                   bank[:, :].rearrange("p (k t) -> p k t", k=KH),
                                                   N_SCALE, dst[0][:, :, :], ALU.mult, ALU.subtract)\
                        .then_inc(S[stage + "_dve"], 1)

                def combine():
                    dve.wait_ge(S["out_pe"], after("out_pe", "y", i - 2))
                    for b in range(GB):
                        nc.vector.scalar_tensor_tensor(xg(i - 2, b), up_p[0][:, b * D:(b + 1) * D],
                                                       mcoef[:, b:b + 1], xg(i - 2, b), ALU.mult, ALU.add)\
                            .then_inc(S["out_dve"], 1)

                def ffn_residual():
                    dve.wait_ge(S["ffn_pe"], after("ffn_pe", "down", i))
                    nc.vector.scalar_tensor_tensor(xg(i), down_p[:, :], unsc[:, 0:1], xg(i),
                                                   ALU.mult, ALU.add).then_inc(S["ffn_dve"], 1)

                def masked(j):
                    g, bank = i - 2, mask_banks(ffn)[j]
                    dve.wait_ge(S["moe_act"], after("moe_act", f"hc{j}", g))
                    dve.wait_ge(S["moe_pe"], after("moe_pe", f"mask{j}", g))
                    nc.vector.tensor_tensor(hm_f[:, 2 * j:2 * j + 2, :], hc[:, 2 * j:2 * j + 2, :],
                                            bank[:, :].rearrange("p (m t) -> p m t", m=2),
                                            ALU.mult).then_inc(S["moe_dve"], 1)

                first, second = (isinstance(i, int) and i == n for n in (0, 1))
                if first:
                    setup_scales()
                if ffn:
                    low(n2h, tp_a, "ffn")
                if first:
                    for n in range(4, PREP):
                        prep_low(n)
                    dve.wait_ge(rest_in, 32)
                if wkv:
                    moments("wkv", 0, i + 1)
                if att and ffn:
                    dve.wait_ge(S["ffn_dve"], after("ffn_dve", "x2", i - 1))
                    moments("att", 2, i - 1)
                if wkv:
                    offsets("wkv", 0, i + 1)
                if last and (ffn or not att):
                    masked(0)
                if att and ffn:
                    offsets("att", 2, i - 1)
                if ffn:
                    inner(0)
                if last and (ffn or not att):
                    masked(1)
                if first:
                    scale_down((0, 1))
                if second:
                    moe_factors()
                if ffn:
                    inner(1)
                if first:
                    scale_down((2, 3))
                    measure_down()
                if wkv:
                    wkv_sums(i + 1)
                if first:
                    down_factors()
                    inner(2)
                    down_low(0)
                    inner(3)
                    down_low(1)
                if wkv:
                    wkv_inverse(0, i + 1)
                if att:
                    s, g = S["att_dve"], i - 1
                    dve.wait_ge(S["att_pe"], after("att_pe", "scores", g))
                    nc.vector.reduce_max(rmax, mix_p[:, 0:GB * T].rearrange("p (b t) -> p b t", b=GB),
                                         AX.X).then_inc(s, 1)
                    dve.wait_ge(s, after("att_dve", "rmax", g))
                    nc.vector.tensor_scalar(nbias, rmax, -(D ** -0.5), None, ALU.mult).then_inc(s, 1)
                    nc.vector.tensor_scalar(valid, rmax, MASKED / 2, tg[:, 1:2], ALU.is_gt, ALU.mult)\
                        .then_inc(s, 1)
                if last and att and not ffn:
                    masked(0)
                    masked(1)
                if ffn and not first:
                    inner(2)
                    inner(3)
                if att:
                    dve.wait_ge(S["att_act"], after("att_act", "exp1", g))
                    nc.vector.reciprocal(rsum, psum_row).then_inc(s, 1)
                    dve.wait_ge(s, after("att_dve", "rsum", g))
                    nc.vector.tensor_tensor(acoef, rsum, valid, ALU.mult).then_inc(s, 1)
                    dve.wait_ge(S["att_pe"], after("att_pe", "pv", g))
                    dve.wait_ge(s, after("att_dve", "coef", g))
                    for b in range(GB):
                        nc.vector.scalar_tensor_tensor(xg(g, b), mix_p[:, b * D:(b + 1) * D],
                                                       acoef[:, b:b + 1], xg(g, b), ALU.mult, ALU.add)\
                            .then_inc(s, 1)
                    dve.wait_ge(s, after("att_dve", "x3_1", g))
                    moments("att", 3, g, "n")
                if second:
                    moe_low_halves((0, 1))
                if wkv:
                    wkv_inverse(1, i + 1)
                if att:
                    offsets("att", 3, g, "n")
                if wkv:
                    wkv_quotient(i + 1)
                if ffn and not first:
                    ffn_residual()
                if ffn and not wkv:
                    dve.wait_ge(S["ffn_dve"], after("ffn_dve", "x2", i))
                    moments("att", 2, i)
                if wkv:
                    wkv_residual(i + 1)
                    dve.wait_ge(S["wkv_dve"], after("wkv_dve", "x1", i + 1))
                    moments("wkv", 1, i + 1, "n")
                if first:
                    ffn_residual()
                if att:
                    if not ffn and last:
                        combine()
                    low(n4h, tp_b, "moe")
                if ffn and not wkv:
                    offsets("att", 2, i)
                if wkv:
                    offsets("wkv", 1, i + 1, "n")
                if first:
                    measure_moe()
                if second:
                    moe_low_halves((2,))
                if last and (ffn or not att):
                    combine()
                if att:
                    s, g = S["moe_dve"], i - 1
                    lg = mix_p[:, 0:GB * EXPERTS].rearrange("p (b e) -> p b e", b=GB)
                    rk = rank[:, :].rearrange("p (b e) -> p b e", b=GB)
                    dve.wait_ge(S["moe_pe"], after("moe_pe", "logits", g))
                    nc.vector.reduce_max(lmax, lg, AX.X).then_inc(s, 1)
                    dve.wait_ge(s, after("moe_dve", "lmax", g))
                    nc.vector.tensor_tensor(diff[:, :, :], lg,
                                            lmax.unsqueeze(2).broadcast_to([P, GB, EXPERTS]),
                                            ALU.subtract).then_inc(s, 1)
                    dve.wait_ge(s, after("moe_dve", "diff", g))
                    nc.vector.scalar_tensor_tensor(ranked[:, :, :], diff[:, :, :], 0.0, rk,
                                                   ALU.is_ge, ALU.mult).then_inc(s, 1)
                    dve.wait_ge(s, after("moe_dve", "ranked", g))
                    nc.vector.reduce_max(rtop, ranked[:, :, :], AX.X).then_inc(s, 1)
                    dve.wait_ge(s, after("moe_dve", "rtop", g))
                    nc.vector.tensor_tensor(onehot[:, :, :], ranked[:, :, :],
                                            rtop.unsqueeze(2).broadcast_to([P, GB, EXPERTS]),
                                            ALU.is_equal).then_inc(s, 1)
                    dve.wait_ge(S["moe_act"], after("moe_act", "exp", g))
                    nc.vector.reduce_sum(msum, pexp[:, :, :], AX.X).then_inc(s, 1)
                    dve.wait_ge(s, after("moe_dve", "rsum", g))
                    nc.vector.reciprocal(mrinv, msum).then_inc(s, 1)
                    dve.wait_ge(s, after("moe_dve", "rinv", g))
                    nc.vector.tensor_scalar(mcoef, mrinv, tg4, None, ALU.mult).then_inc(s, 1)
            pipeline(dve, run)

        @block.tensor
        def _(pe):
            def to_channels(dst, src):
                for k in range(KH):
                    for b in range(GB):
                        c = k * TW + b * T
                        last = nc.tensor.transpose(dst[:, c:c + T], src[:, b, k * P:(k + 1) * P], ident[:, :])
                return last

            def y_to_tokens():
                for b in range(GB):
                    for k in range(KH):
                        last = nc.tensor.transpose(tp_a[:, b * D + k * P:b * D + (k + 1) * P],
                                                   y_t[:, k * TW + b * T:k * TW + (b + 1) * T], ident[:, :])
                return last

            def split_matmul(dst, lhs, rhs, first, last):
                for n, (a, b) in enumerate(((0, 0), (1, 0), (0, 1))):
                    o = nc.tensor.matmul(dst, lhs(a), rhs(b), start=first and n == 0, stop=last and n == 2)
                return o

            def prep(n):
                w, half, c = chunk(n)
                for k in range(KH):
                    sign = P if half and k else 0
                    last = nc.tensor.matmul(prep_bank[n][:, :], had[:, sign:sign + P],
                                            (raw_up, raw_gate)[w][:, k, c * 512:(c + 1) * 512],
                                            start=k == 0, stop=k == 1)
                last.then_inc(prep_pe, 1)

            pe.wait_ge(consts_in, 32)
            pe.wait_ge(S["wkv_act"], after("wkv_act", "norm1", 0))
            to_channels(tp_a, n1).then_inc(S["wkv_pe"], 1)
            pe.wait_ge(up_in, 16)
            for n in by_arrival[:4]:
                prep(n)
            pe.wait_ge(gate_in, 16)
            prep(by_arrival[4])
            pe.wait_ge(S["wkv_act"], after("wkv_act", "e2_1", 0))
            pe.wait_ge(S["wkv_dve"], after("wkv_dve", "y", 0))
            y_to_tokens().then_inc(S["wkv_pe"], 1)
            prep(by_arrival[5])
            prep(by_arrival[6])
            pe.wait_ge(prep_lo, 2)
            prep(by_arrival[7])

            def transform_down(blocks):
                pe.wait_ge(bfly_done, 6)
                for j in blocks:
                    if j == 3:
                        pe.wait_ge(down_f32, 2)
                    o = nc.tensor.matmul(down_bank[j][:, :], had[:, 0:P],
                                         bfly[:, 2 * j:2 * j + 2, :], start=True, stop=True)
                    o.then_inc(prep_down, 1)

            def run(i, ffn, wkv, att, last):
                def inner_product(w, p):
                    dst, weights, user = ((gate_p, gate_h, "z"), (up_p, up_h, "h"))[w]
                    if p >= 2:
                        pe.wait_ge(S["ffn_dve"], after("ffn_dve", f"{user}{p - 2}", i))
                    elif w == 0 and last:
                        pe.wait_ge(S["moe_act"], after("moe_act", f"hc{p}", i - 2))
                    for m in (2 * p, 2 * p + 1):
                        for k in range(KH):
                            o = split_matmul(dst[p % 2][:, m % 2 * TW:(m % 2 + 1) * TW],
                                             lambda a: weights[a][:, k, m * P:(m + 1) * P],
                                             lambda a: n2h[a][:, k, :], k == 0, k == KH - 1)
                    o.then_inc(S["ffn_pe"], 1)

                def ranks(j):
                    for m in (2 * j, 2 * j + 1):
                        for k in range(KH):
                            o = split_matmul(gate_p[j][:, m % 2 * TW:(m % 2 + 1) * TW],
                                             lambda a: a_h[a][:, k, m * P:(m + 1) * P],
                                             lambda a: n4h[a][:, k, :], k == 0, k == KH - 1)
                    o.then_inc(S["moe_pe"], 1)

                def mask(j, bank):
                    for m in (2 * j, 2 * j + 1):
                        o = nc.tensor.matmul(bank[:, m % 2 * TW:(m % 2 + 1) * TW],
                                             expand[:, m * P:(m + 1) * P], onehotT[:, :, :],
                                             start=True, stop=True)
                    o.then_inc(S["moe_pe"], 1)

                def down(b, steps):
                    for a, m in steps:
                        if first and b == a == 0 and m % (MI // 2) == 0:
                            pe.wait_ge(down_lo, m // (MI // 2) + 1)
                        if b == 0 and m % 2 == 0:
                            if a == 0:
                                pe.wait_ge(S["ffn_act"], after("ffn_act", f"hhi{m // 2}", i))
                            else:
                                pe.wait_ge(S["ffn_pool"], after("ffn_pool", f"hlo{m // 2}", i))
                        for w in range(2 - a):
                            o = nc.tensor.matmul(down_p[:, b * D:(b + 1) * D],
                                                 h_h[a][:, m, b * T:(b + 1) * T], down_h[w][:, m, :],
                                                 start=a == w == m == 0, stop=(a, m) == DOWN_STEPS[-1])
                    return o

                first, second = (isinstance(i, int) and i == n for n in (0, 1))
                g, e = i - 1, i - 2

                def queries():
                    if second:
                        pe.wait_ge(small_ready, 3)
                        pe.wait_ge(small_in, 16 * 6)
                    pe.wait_ge(S["att_act"], after("att_act", "norm1", g))
                    if last and ffn:
                        pe.wait_ge(S["moe_dve"], after("moe_dve", "hm1", e))
                    to_channels(tp_b, n3).then_inc(S["att_pe"], 1)

                def scores():
                    pe.wait_ge(S["att_act"], after("att_act", "nT", g))
                    if not ffn:
                        pe.wait_ge(S["moe_dve"], after("moe_dve", "diff", e))
                    for b in range(GB):
                        for k in range(KH):
                            nc.tensor.matmul(mix_p[:, b * T:(b + 1) * T], n3T[:, k, b * T:(b + 1) * T],
                                             v_all[:, bass.ds(g * GW + k * TW + b * T, T)],
                                             start=k == 0, stop=False)
                        o = nc.tensor.matmul(mix_p[:, b * T:(b + 1) * T], ones[:, :],
                                             mask_b[:, bass.ds(g * TW + b * T, T)],
                                             start=False, stop=True)
                    o.then_inc(S["att_pe"], 1)

                def weights_transposed():
                    pe.wait_ge(S["att_act"], after("att_act", "exp1", g))
                    for b in range(GB):
                        o = nc.tensor.transpose(tp_b[:, b * T:(b + 1) * T], prob[:, b, :], ident[:, :])
                    o.then_inc(S["att_pe"], 1)

                def readout():
                    if second:
                        pe.wait_ge(ctx_in, 16)
                    pe.wait_ge(S["att_act"], after("att_act", "pT", g))
                    for b in range(GB):
                        o = nc.tensor.matmul(mix_p[:, b * D:(b + 1) * D], probT[:, b, :],
                                             c_all[:, bass.ds(g * GW + b * D, D)], start=True, stop=True)
                    o.then_inc(S["att_pe"], 1)

                def experts_input():
                    if second:
                        pe.wait_ge(moe_lo, 2)
                    pe.wait_ge(S["att_act"], after("att_act", "norm1n", g))
                    to_channels(tp_b, n4).then_inc(S["moe_pe"], 1)

                def logits():
                    pe.wait_ge(S["moe_dve"], after("moe_dve", "lo", g))
                    for b in range(GB):
                        for k in range(KH):
                            o = split_matmul(mix_p[:, b * EXPERTS:(b + 1) * EXPERTS],
                                             lambda a: n4h[a][:, k, b * T:(b + 1) * T],
                                             lambda a: wg_h[a][:, k, :], k == 0, k == KH - 1)
                    o.then_inc(S["moe_pe"], 1)

                def choice():
                    pe.wait_ge(S["moe_dve"], after("moe_dve", "onehot", e))
                    for b in range(GB):
                        o = nc.tensor.transpose(choice_bank(ffn)[0:EXPERTS, b * T // 2:(b + 1) * T // 2].bitcast(bf16),
                                                onehot[:, b, :], ident_b[:, :])
                    o.then_inc(S["moe_pe"], 1)

                def masks():
                    pe.wait_ge(S["moe_act"], after("moe_act", "ohT", e))
                    for j, bank in enumerate(mask_banks(ffn)):
                        mask(j, bank)

                def experts_output():
                    for b in range(GB):
                        for a, m in B_STEPS:
                            if b == 0 and m % 2 == 0:
                                if a == 0:
                                    pe.wait_ge(S["moe_act"], after("moe_act", f"mhi{m // 2}", e))
                                else:
                                    pe.wait_ge(S["moe_pool"], after("moe_pool", f"mlo{m // 2}", e))
                            for w in range(2 - a):
                                o = nc.tensor.matmul(up_p[0][:, b * D:(b + 1) * D],
                                                     hm_h[a][:, m, b * T:(b + 1) * T], b_h[w][:, m, :],
                                                     start=a == w == m == 0, stop=(a, m) == B_STEPS[-1])
                    o.then_inc(S["out_pe"], 1)

                def wkv_output():
                    pe.wait_ge(S["wkv_dve"], after("wkv_dve", "y", i + 1))
                    y_to_tokens().then_inc(S["wkv_pe"], 1)

                if not ffn:
                    if att:
                        queries()
                    if last:
                        choice()
                        ranks(1)
                    if att:
                        scores()
                    if last:
                        masks()
                    if att:
                        weights_transposed()
                        readout()
                    if last:
                        experts_output()
                    if att:
                        experts_input()
                        logits()
                        ranks(0)
                    return

                pe.wait_ge(S["wkv_act"], after("wkv_act", "norm1n", i))
                to_channels(tp_a, n2).then_inc(S["ffn_pe"], 1)
                if last:
                    choice()
                    ranks(1)
                if first:
                    pe.wait_ge(prep_lo, 4)
                pe.wait_ge(S["ffn_dve"], after("ffn_dve", "lo", i))
                inner_product(0, 0)
                if last:
                    masks()
                inner_product(1, 0)
                if first:
                    pe.wait_ge(prep_lo, PREP)
                inner_product(0, 1)
                if first:
                    transform_down((0, 1, 2))
                if wkv:
                    pe.wait_ge(S["wkv_act"], after("wkv_act", "norm1", i + 1))
                    to_channels(tp_a, n1).then_inc(S["wkv_pe"], 1)
                inner_product(1, 1)
                if first:
                    transform_down((3,))
                if att:
                    queries()
                inner_product(0, 2)
                inner_product(1, 2)
                if att:
                    scores()
                inner_product(0, 3)
                inner_product(1, 3)
                if att:
                    weights_transposed()
                down(0, DOWN_STEPS[:3])
                if att:
                    readout()
                down(0, DOWN_STEPS[3:])
                if first:
                    wkv_output()
                down(1, DOWN_STEPS).then_inc(S["ffn_pe"], 1)
                if wkv and not first:
                    wkv_output()
                if att:
                    experts_input()
                if last:
                    experts_output()
                if att:
                    logits()
                    ranks(0)
                if second:
                    pe.wait_ge(moe_lo, 3)
            pipeline(pe, run)


def kernel(x, ctx_2048, mask_BxS2_bk0, g_xattn, g_ffn, L0_xattn_time_decay, L0_xattn_time_first,
           L0_ffn_SU_ug, L0_ffn_SU_dp, L0_ffn_Wscale_ug, L0_ffn_Wscale_dp, L0_ffn_W_up,
           L0_ffn_W_gate, L0_ffn_W_down, L1_ffn_A, L1_ffn_Bw, L1_ffn_Wg):
    import numpy as np
    import concourse.bacc as bacc
    from concourse.bass_utils import run_bass_kernel_spmd

    c = np.ascontiguousarray

    def chunks(a):
        return c(a.reshape(a.shape[0] // P, P, a.shape[1]).transpose(1, 0, 2))

    def cols(v):
        return np.asarray(v).reshape(-1, P).T

    x, ctx = np.asarray(x), np.asarray(ctx_2048)
    gates = np.concatenate([np.asarray(g_xattn), np.asarray(g_ffn)])
    wug = np.asarray(L0_ffn_Wscale_ug)
    vecs = np.concatenate([
        cols(L0_xattn_time_decay), cols(L0_xattn_time_first), cols(L0_ffn_SU_ug), cols(L0_ffn_SU_dp),
        cols(wug[INTER:]), cols(wug[:INTER]), np.broadcast_to(gates, (P, 4)),
        np.broadcast_to(np.asarray(L0_ffn_Wscale_dp), (P, D))], axis=1)
    had = np.ones((1, 1), np.float32)
    while had.shape[0] < P:
        had = np.block([[had, had], [had, -had]])
    arrays = {
        "x_tok": c(x.transpose(1, 0, 2)).reshape(P, B * D),
        "ctx_tok": c(ctx.transpose(1, 0, 2)).reshape(P, B * D),
        "ctx_chan": c(ctx.reshape(GROUPS, GB, T, KH, P).transpose(4, 0, 3, 1, 2)).reshape(P, -1),
        "mask_row": np.asarray(mask_BxS2_bk0).reshape(1, B * T),
        "vecs": c(vecs),
        "w_up_t": chunks(np.asarray(L0_ffn_W_up).T),
        "w_gate_t": chunks(np.asarray(L0_ffn_W_gate).T),
        "w_down_t": chunks(np.asarray(L0_ffn_W_down).T),
        "a_t": chunks(np.asarray(L1_ffn_A).reshape(ER, D).T),
        "b_t": chunks(np.asarray(L1_ffn_Bw).transpose(0, 2, 1).reshape(ER, D)),
        "wg_t": chunks(np.asarray(L1_ffn_Wg).T),
        "hadamard": np.concatenate([had, -had], axis=1).astype(np.float32),
        "ident_in": np.eye(P, dtype=np.float32),
        "expand_in": np.repeat(np.eye(EXPERTS, dtype=np.float32), RANK, axis=1),
        "rank_in": np.broadcast_to(
            np.arange(EXPERTS, 0, -1, dtype=np.float32), (P, GB, EXPERTS)).reshape(P, -1).copy(),
    }
    nc = bacc.Bacc("TRN2", target_bir_lowering=False, num_devices=1)
    args = [nc.dram_tensor(n, a.shape, mybir.dt.from_np(a.dtype), kind="ExternalInput").ap()
            for n, a in arrays.items()]
    out = nc.dram_tensor("out_tok", (P, B * D), mybir.dt.float32, kind="ExternalOutput").ap()
    flamingo_kernel(nc, *args, out)
    r = run_bass_kernel_spmd(nc, [arrays], core_ids=[0])
    got = r.results[0]["out_tok"]
    return c(np.asarray(got).reshape(T, B, D).transpose(1, 0, 2))
```
